# Optimizing a Trainium2 kernel written in Bass

```python
import numpy as np
import jax
import jax.numpy as jnp

def _softmax(x, axis=-1):
    return jax.nn.softmax(x, axis=axis)

def _gelu(x):
    return jax.nn.gelu(x, approximate=True)

def _silu(x):
    return jax.nn.silu(x)

def _sigmoid(x):
    return jax.nn.sigmoid(x)

def _layernorm(x, axis=-1, eps=1e-05):
    m = jnp.mean(x, axis=axis, keepdims=True)
    v = jnp.var(x, axis=axis, keepdims=True)
    return (x - m) / jnp.sqrt(v + eps)

def _scatter_add(tgt, idx, src, axis=0):
    return tgt.at[idx].add(src)

def _segment_sum(src, seg, n):
    return jax.ops.segment_sum(src, seg, n)
kernel_name = 'mk_recurrent_d1_jaxref_r8_d6ab42'

def setup_inputs(seed: int=0):
    np.random.seed(seed)
    _w = jnp.asarray

    def _L0_attn_setup():
        import jax, jax.numpy as jnp
        import numpy as np
        B, L, D, DIN, S, R, K = (2, 128, 128, 256, 16, 64, 4)
        key = jax.random.key(seed)
        ks = jax.random.split(key, 8)
        f = lambda k, sh, sc: jax.random.normal(k, sh, jnp.float32) * sc
        return {'x': f(ks[0], (B, L, D), 1.0), 'norm_w': jnp.ones((D,), jnp.float32), 'W_in': f(ks[1], (D, 2 * DIN), D ** (-0.5)), 'conv_w': f(ks[2], (DIN, 1, K), 0.5), 'conv_b': jnp.zeros((DIN,), jnp.float32), 'W_x': f(ks[3], (DIN, R + 2 * S), DIN ** (-0.5)), 'W_dt': f(ks[4], (R, DIN), R ** (-0.5)), 'b_dt': f(ks[5], (DIN,), 0.1), 'A_log': jnp.log(jnp.broadcast_to(jnp.arange(1, S + 1, dtype=jnp.float32), (DIN, S))), 'D_skip': jnp.ones((DIN,), jnp.float32), 'W_out': f(ks[6], (DIN, D), DIN ** (-0.5))}
    _L0_attn_in = _L0_attn_setup()

    def _L0_ffn_setup():
        import jax, jax.numpy as jnp
        import numpy as np
        E = 8
        D = 128
        H = 256
        TOP_K = 2
        key = jax.random.key(seed)
        k_x, k_g, k_w1, k_w2 = jax.random.split(key, 4)
        B, S = (4, 256)
        inp = {'input': jax.random.normal(k_x, (B, S, D), dtype=jnp.float32), 'Wg': jax.random.normal(k_g, (D, E), dtype=jnp.float32) * 0.02, 'W1': jax.random.normal(k_w1, (E, D, H), dtype=jnp.float32) * 0.02, 'b1': jnp.zeros((E, H), dtype=jnp.float32), 'W2': jax.random.normal(k_w2, (E, H, D), dtype=jnp.float32) * 0.02, 'b2': jnp.zeros((E, D), dtype=jnp.float32)}
        return inp
    _L0_ffn_in = _L0_ffn_setup()
    _d = {'L0_attn_x': _L0_attn_in['x'], 'L0_attn_norm_w': _L0_attn_in['norm_w'], 'L0_attn_W_in': _L0_attn_in['W_in'], 'L0_attn_conv_w': _L0_attn_in['conv_w'], 'L0_attn_conv_b': _L0_attn_in['conv_b'], 'L0_attn_W_x': _L0_attn_in['W_x'], 'L0_attn_W_dt': _L0_attn_in['W_dt'], 'L0_attn_b_dt': _L0_attn_in['b_dt'], 'L0_attn_A_log': _L0_attn_in['A_log'], 'L0_attn_D_skip': _L0_attn_in['D_skip'], 'L0_attn_W_out': _L0_attn_in['W_out'], 'L0_ffn_Wg': _L0_ffn_in['Wg'], 'L0_ffn_W1': _L0_ffn_in['W1'], 'L0_ffn_b1': _L0_ffn_in['b1'], 'L0_ffn_W2': _L0_ffn_in['W2'], 'L0_ffn_b2': _L0_ffn_in['b2']}
    _x0 = _d['L0_attn_x']
    _d['L0_attn_x'] = jax.random.normal(jax.random.fold_in(jax.random.key(seed), 1), (8, 256, 128), dtype=_x0.dtype)
    del _x0
    return _d

def reference(L0_attn_x, L0_attn_norm_w, L0_attn_W_in, L0_attn_conv_w, L0_attn_conv_b, L0_attn_W_x, L0_attn_W_dt, L0_attn_b_dt, L0_attn_A_log, L0_attn_D_skip, L0_attn_W_out, L0_ffn_Wg, L0_ffn_W1, L0_ffn_b1, L0_ffn_W2, L0_ffn_b2):

    def _L0_attn_ref(x, norm_w, W_in, conv_w, conv_b, W_x, W_dt, b_dt, A_log, D_skip, W_out):
        import jax, jax.numpy as jnp
        import numpy as np
        B, L, D, DIN, S, R, K = (2, 128, 128, 256, 16, 64, 4)
        eps = 1e-05
        xn = x * jax.lax.rsqrt(jnp.mean(x * x, axis=-1, keepdims=True) + eps) * norm_w
        xz = xn @ W_in
        xi, z = jnp.split(xz, 2, axis=-1)
        xt = jnp.transpose(xi, (0, 2, 1))
        xc = jax.lax.conv_general_dilated(xt, conv_w, (1,), [(K - 1, 0)], feature_group_count=DIN)
        xc = jnp.transpose(xc, (0, 2, 1)) + conv_b
        xc = jax.nn.silu(xc)
        xd = xc @ W_x
        dt, Bm, Cm = jnp.split(xd, [R, R + S], axis=-1)
        dt = jax.nn.softplus(dt @ W_dt + b_dt)
        A = -jnp.exp(A_log)
        dA = jnp.exp(dt[..., None] * A)
        dBu = (dt * xc)[..., None] * Bm[:, :, None, :]

        def comb(c1, c2):
            a1, b1 = c1
            a2, b2 = c2
            return (a1 * a2, a2 * b1 + b2)
        _, h = jax.lax.associative_scan(comb, (dA, dBu), axis=1)
        y = jnp.einsum('blds,bls->bld', h, Cm) + D_skip * xc
        y = y * jax.nn.silu(z)
        return x + y @ W_out

    def _L0_ffn_ref(input, Wg, W1, b1, W2, b2):
        import jax, jax.numpy as jnp
        import numpy as np
        E = 8
        D = 128
        H = 256
        TOP_K = 2
        logits = jnp.einsum('bsd,de->bse', input, Wg)
        probs = jax.nn.softmax(logits, axis=-1)
        top_vals, top_idx = jax.lax.top_k(probs, TOP_K)
        top_vals = top_vals / jnp.sum(top_vals, axis=-1, keepdims=True)
        onehot = jax.nn.one_hot(top_idx, E, dtype=input.dtype)
        mask = jnp.sum(onehot, axis=2)
        scores = jnp.sum(onehot * top_vals[..., None], axis=2)
        xm = input[None] * jnp.moveaxis(mask, -1, 0)[..., None]
        h = jnp.einsum('ebsd,edh->ebsh', xm, W1) + b1[:, None, None, :]
        h = jax.nn.relu(h)
        y = jnp.einsum('ebsh,ehd->ebsd', h, W2) + b2[:, None, None, :]
        out = jnp.sum(y * jnp.moveaxis(scores, -1, 0)[..., None], axis=0)
        return out
    x = L0_attn_x
    xn = _layernorm(x, axis=-1)
    s = _L0_attn_ref(xn, L0_attn_norm_w, L0_attn_W_in, L0_attn_conv_w, L0_attn_conv_b, L0_attn_W_x, L0_attn_W_dt, L0_attn_b_dt, L0_attn_A_log, L0_attn_D_skip, L0_attn_W_out)
    g = _silu(_L0_ffn_ref(xn, L0_ffn_Wg, L0_ffn_W1, L0_ffn_b1, L0_ffn_W2, L0_ffn_b2))
    x = x + s * g
    return x

_drawn_inputs = setup_inputs


def setup_inputs(seed=0):
    import zlib

    import numpy as np

    out = dict(_drawn_inputs(seed))
    spreads = {'L0_attn_norm_w': (1.0, 0.6),
     'L0_attn_conv_b': (0.0, 0.8),
     'L0_attn_D_skip': (1.0, 0.6),
     'L0_ffn_b1': (0.0, 0.77),
     'L0_ffn_b2': (0.0, 0.1)}
    factors = {'L0_attn_W_dt': 4.717, 'L0_attn_b_dt': 8.0, 'L0_attn_A_log': 8.0}
    for name, (base, spread) in spreads.items():
        noise = np.random.default_rng([zlib.crc32(name.encode()), seed]).standard_normal(out[name].shape)
        drawn = base * np.exp(spread * noise) if base else spread * noise
        out[name] = jnp.asarray(drawn.astype(out[name].dtype))
    for name, factor in factors.items():
        out[name] = (out[name] * factor).astype(out[name].dtype)
    return out
```

```python
from contextlib import ExitStack

import concourse.bass as bass
from concourse import mybir

ALU = mybir.AluOpType
ACT = mybir.ActivationFunctionType
AX = mybir.AxisListType
F32 = mybir.dt.float32
BF16 = mybir.dt.bfloat16
U32 = mybir.dt.uint32

P = 128
BATCH, SEQ, D = 8, 256, 128
DIN, STATES, RANK, TAPS = 256, 16, 64, 4
EXPERTS, HID = 8, 256
EPS = 1e-5
TOK = BATCH * SEQ
CH = 512
BPC = CH // SEQ
TPC = CH // P
CHUNKS = TOK // CH
DB = DIN // P
GD = P // STATES
GL = 32 // GD
NQ = P // 32
UNITS = DB * GL * NQ
PACK = NQ
HB = HID // P
PAD = TAPS - 1
FAR = 1.0e28

V_A, V_B1, V_BDT, V_CB, V_DS, V_NW, V_END = 0, 32, 48, 50, 52, 54, 55

PRE_JOBS = ["tn", "tr", "z0", "z1", "gl", "xc0", "xc1", "dt", "B", "C", "gs", "gb", "v0", "v1", "nop"]
EMPTIED_BY_DVE = {"gl", "o"} | {f"y{e}" for e in range(EXPERTS)}
SLOTS = {
    0: ["m0a"], 1: ["m0b"], 2: ["tn"], 3: ["tr", "y0"],
    4: ["m1a"], 5: ["z0", "z1"], 6: ["m1b", "gl"], 7: ["xc0"], 8: ["xc1"],
    9: ["y1"], 10: ["m2a", "m2b"], 11: ["dt"], 12: ["B", "gs"], 13: ["C", "gb"], 14: ["v0", "v1"],
    15: ["y2"], 16: ["m3a"], 17: ["m3b"], 18: ["y3"], 19: ["m4a"], 20: ["m4b"], 21: ["y4"],
    22: ["m5a"], 23: ["m5b"], 24: ["y5"], 25: ["m6a"], 26: ["m6b"], 27: ["y6"],
    28: ["m7a"], 29: ["m7b"], 30: ["y7"], 31: ["nop", "nop2", "nop3"],
}
PERIOD_JOBS = [j for n in range(UNITS) for j in SLOTS[n]] + ["o"]
GATE_STEPS = 14
AUX = 3
REDUCE_AT = {4 * m + 5: m for m in range(UNITS // PACK - 1)}


def emptied(jobs, name=None):
    upto = jobs if name is None else jobs[:jobs.index(name) + 1]
    v = sum(j in EMPTIED_BY_DVE for j in upto)
    return len(upto) - v, v


def mamba_moe(nc, x, norm_w, W_in, conv_w, conv_b, W_x, W_dt, b_dt, A_log, D_skip, W_out,
              Wg, W1, b1, W2, b2, out):
    last_jobs = [j for j in PERIOD_JOBS if j not in PRE_JOBS and j[:3] != "nop"]
    assert len(PRE_JOBS) % AUX == 0 and len(PERIOD_JOBS) % AUX == 0, (len(PRE_JOBS), len(PERIOD_JOBS))

    with ExitStack() as ctx:
        def sb(name, shape, dt=F32):
            return ctx.enter_context(nc.sbuf_tensor(name, shape, dt))

        def sem(name):
            return ctx.enter_context(nc.semaphore(name))

        x_sb = sb("x_sb", [P, CHUNKS, TPC, D])
        xn = sb("xn", [P, CHUNKS, TPC, D])
        acc = sb("acc", [P, CHUNKS, CH])
        s_sb = xn[:, :, :, :].rearrange("p c t d -> p c (t d)")
        xr = sb("xr", [P, TPC, D])
        sq = sb("sq", [P, TPC, D])
        xnT_next = sb("xnT_next", [P, CH])
        xnT = sb("xnT", [P, CH])
        xrT = sb("xrT", [P, BPC, PAD + SEQ])
        zr = sb("zr", [P, DB, CH])
        xv = sb("xv", [P, DB, CH])
        sz = sb("sz", [P, 2, DB, CH])
        xc = sb("xc", [P, 2, DB, CH])
        Bt = sb("Bt", [P, 2, CH])
        Ct = sb("Ct", [P, 2, CH])
        dtp = sb("dtp", [P, CH])
        ev = sb("ev", [P, DB, CH])
        rl = sb("rl", [P, DB, CH])
        lg1p, corr = zr, xv
        parts = sb("parts", [P, DB, 2, 3, CH])
        stack = sb("stack", [P, DB, NQ, 2, CH])
        win = sb("win", [P, 2 * DIN])
        wtap = sb("wtap", [P, TAPS, DIN])
        cwb = parts[:, 0, 0, 0:2, :].rearrange("p a b -> p (a b)").rearrange("p (d k) -> p d k", k=TAPS)
        wx = sb("wx", [P, DB, RANK + 2 * STATES])
        wB = sb("wB", [P, DB, GD, STATES])
        wC = sb("wC", [P, DB, GD, STATES])
        wR = sb("wR", [P, DB, P])
        wdt = sb("wdt", [P, DIN])
        wout = sb("wout", [P, DB, D])
        wg = sb("wg", [P, EXPERTS])
        w1 = sb("w1", [P, EXPERTS, HID])
        w2 = sb("w2", [P, EXPERTS, HB, D])
        b2d = sb("b2d", [TPC * EXPERTS, TPC, D])
        rows = sb("rows", [V_END, P])
        cols = sb("cols", [P, V_END])
        negA = sb("negA", [P, 32])
        ident = sb("ident", [P, P])
        own = sb("own", [P, GD])
        sel = sb("sel", [96, GL, GD, STATES], BF16)
        rsel = sb("rsel", [P, GL, 32])
        iota8 = sb("iota8", [P, TPC, EXPERTS])
        mhalf = sb("mhalf", [P, TPC])
        st = sb("st", [P, TPC, 6])
        mv = sb("mv", [P, TPC, 2])
        nops = sb("nops", [P, len(PRE_JOBS) + CHUNKS * len(PERIOD_JOBS)])
        ve = sb("ve", [P, TPC])
        rstd = sb("rstd", [P, TPC])
        ms = sb("ms", [P, TPC])
        me = sb("me", [P, TPC])
        rr = sb("rr", [P, TPC])
        gmx = sb("gmx", [P, TPC])
        glc = sb("glc", [P, TPC, EXPERTS])
        gex = sb("gex", [P, TPC, EXPERTS])
        gsm = sb("gsm", [P, TPC])
        gri = sb("gri", [P, TPC])
        gp = sb("gp", [P, TPC, EXPERTS])
        gv8 = sb("gv8", [P, TPC, 8])
        gi8 = sb("gi8", [P, TPC, 8], U32)
        gif = sb("gif", [P, TPC, 2])
        gs2 = sb("gs2", [P, TPC])
        grs = sb("grs", [P, TPC])
        gvn = sb("gvn", [P, TPC, 2])
        goh = sb("goh", [P, 2, TPC, EXPERTS])
        gw = sb("gw", [P, 2, TPC, EXPERTS])
        score = sb("score", [P, 2, TPC, EXPERTS])
        sT = sb("sT", [TPC * EXPERTS, P])
        dbu = sb("dbu", [P, 2, CH])
        hs = sb("hs", [P, 3, CH])
        hc = sb("hc", [P, 2 * PACK, CH])
        hT = sb("hT", [P, 2, HB, CH])
        yg = sb("yg", [P, DB, CH])

        def bank(name):
            return ctx.enter_context(nc.psum_tensor(name, [P, CH], F32))

        pd = [bank(f"pd{i}") for i in range(2)]
        pu = [bank(f"pu{i}") for i in range(2)]
        py = bank("py")
        px = [bank(f"px{i}") for i in range(AUX)]

        x_first, x_rest = sem("x_first"), sem("x_rest")
        w_in, w_moe = sem("w_in"), sem("w_moe")
        consts = sem("consts")
        setup = sem("setup")
        vec_t, vec_c, expA = sem("vec_t"), sem("vec_c"), sem("expA")
        ln_mv, ln_ve, ln_rstd, ln_xn = sem("ln_mv"), sem("ln_ve"), sem("ln_rstd"), sem("ln_xn")
        ln_st = sem("ln_st")
        rms_ms, rms_me, rms_r, rms_xr = sem("rms_ms"), sem("rms_me"), sem("rms_r"), sem("rms_xr")
        silu_done = sem("silu_done")
        e_done, l_done = sem("e_done"), sem("l_done")
        round_done, corr_done, lsum_done, dt_done = sem("round_done"), sem("corr_done"), sem("lsum_done"), sem("dt_done")
        u_done, far_done, r1_done, parts_done = sem("u_done"), sem("far_done"), sem("r1_done"), sem("parts_done")
        stacked = [sem("stacked0"), sem("stacked1")]
        gate_exp, gate_step, score_done = sem("gate_exp"), sem("gate_step"), sem("score_done")
        xnT_copied = sem("xnT_copied")
        filled = sem("filled")
        act_emptied, dve_emptied = sem("act_emptied"), sem("dve_emptied")
        dt_spread, u_spread = sem("dt_spread"), sem("u_spread")
        decay_done, dbu_done, scan_done, hc_done = sem("decay_done"), sem("dbu_done"), sem("scan_done"), sem("hc_done")
        reduced = sem("reduced")
        y_taken, yg_done = sem("y_taken"), sem("yg_done")
        moe_acc = sem("moe_acc")
        g_done, sg_done, o_done, stored = sem("g_done"), sem("sg_done"), sem("o_done"), sem("stored")

        xv_dram = x.rearrange("b (h p) d -> p (b h) d", p=P)
        ov_dram = out.rearrange("b (h p) d -> p (b h) d", p=P)
        N_WIN, N_WMOE = 12, 3

        PA, PV = emptied(PRE_JOBS)
        QA, QV = emptied(PERIOD_JOBS)
        NPRE, NPER = len(PRE_JOBS), len(PERIOD_JOBS)

        def base(c):
            return (0, 0, 0) if c < 0 else (NPRE + c * NPER, PA + c * QA, PV + c * QV)

        def jobs_of(c):
            return PRE_JOBS if c < 0 else (PERIOD_JOBS if c < CHUNKS - 1 else last_jobs)

        def bank_of(c, job):
            return px[jobs_of(c).index(job) % AUX]

        def wait_filled(eng, c, job):
            eng.wait_ge(filled, base(c)[0] + jobs_of(c).index(job) + 1)

        def wait_emptied(eng, c, job):
            a, v = emptied(jobs_of(c), job)
            if job in EMPTIED_BY_DVE:
                eng.wait_ge(dve_emptied, base(c)[2] + v)
            else:
                eng.wait_ge(act_emptied, base(c)[1] + a)

        block = ctx.enter_context(nc.Block())

        @block.sync
        def _(sp):
            sp.dma_start(x_sb[:, 0], xv_dram[:, 0:TPC, :]).then_inc(x_first, 16)
            sp.dma_start(win[:, :], W_in[:, :]).then_inc(w_in, 16)
            sp.dma_start(rows[V_A:V_A + 32, :], A_log.rearrange("(g d) s -> g (d s)", d=GD)).then_inc(w_in, 16)
            sp.dma_start(rows[V_B1:V_B1 + 16, :], b1.rearrange("e (b p) -> (e b) p", p=P)).then_inc(w_in, 16)
            sp.dma_start(rows[V_BDT:V_BDT + 2, :], b_dt.rearrange("(b p) -> b p", p=P)).then_inc(w_in, 16)
            sp.dma_start(rows[V_CB:V_CB + 2, :], conv_b.rearrange("(b p) -> b p", p=P)).then_inc(w_in, 16)
            sp.dma_start(rows[V_DS:V_DS + 2, :], D_skip.rearrange("(b p) -> b p", p=P)).then_inc(w_in, 16)
            sp.dma_start(rows[V_NW:V_NW + 1, :], norm_w.rearrange("(b p) -> b p", p=P)).then_inc(w_in, 16)
            sp.dma_start(parts[:, 0, 0, 0:2, :].rearrange("p a b -> p (a b)"),
                         conv_w.rearrange("d a k -> a (d k)").to_broadcast([P, DIN * TAPS])).then_inc(w_in, 16)
            sp.dma_start(wx[:, :, :], W_x.rearrange("(b p) n -> p b n", p=P)).then_inc(w_in, 16)
            sp.dma_start(wdt[0:RANK, :], W_dt[:, :]).then_inc(w_in, 16)
            sp.dma_start(wout[:, :, :], W_out.rearrange("(b p) n -> p b n", p=P)).then_inc(w_in, 16)
            sp.dma_start(wg[:, :], Wg[:, :]).then_inc(w_in, 16)
            sp.dma_start(x_sb[:, 1:CHUNKS], xv_dram[:, TPC:CHUNKS * TPC, :].rearrange("p (c t) d -> p c t d", t=TPC)).then_inc(x_rest, 16)
            sp.dma_start(w1[:, :, :], W1.rearrange("e d h -> d e h")).then_inc(w_moe, 16)
            sp.dma_start(w2[:, :, :, :], W2.rearrange("e (b p) d -> p e b d", p=P)).then_inc(w_moe, 16)
            sp.wait_ge(consts, 2)
            for i in range(TPC):
                sp.dma_start(b2d[i * EXPERTS:(i + 1) * EXPERTS, i, :], b2[:, :]).then_inc(w_moe, 16)

            def restack(k):
                sp.wait_ge(parts_done, k + 1)
                for b in range(DB):
                    if k > 0:
                        sp.wait_ge(u_spread, UNITS * (k - 1) + (b + 1) * UNITS // DB)
                    for p in range(3):
                        for q in range(NQ):
                            sp.dma_start(stack[32 * p:32 * p + 32, b, q, :, :],
                                         parts[32 * q:32 * q + 32, b, :, p, :]).then_inc(stacked[b], 16)

            for k in range(CHUNKS):
                restack(k)
            for k in range(CHUNKS):
                sp.wait_ge(o_done, k + 1)
                sp.dma_start(ov_dram[:, k * TPC:(k + 1) * TPC, :],
                             xn[:, k]).then_inc(stored, 16)
            sp.wait_ge(stored, 16 * CHUNKS)

        @block.gpsimd
        def _(pool):
            pool.memset(ident[:, :], 0.0).then_inc(consts, 1)
            pool.memset(b2d[:, :, :], 0.0).then_inc(consts, 1)
            pool.memset(mhalf[:, :], -0.5).then_inc(consts, 1)
            pool.memset(own[:, :], 1.0).then_inc(consts, 1)
            pool.wait_ge(consts, 4)
            pool.affine_select(out=ident[:, :], in_=ident[:, :], compare_op=ALU.not_equal, fill=1.0,
                               base=0, pattern=[[-1, P]], channel_multiplier=1).then_inc(consts, 1)
            pool.affine_select(out=own[:, :], in_=own[:, :], compare_op=ALU.is_ge, fill=0.0,
                               base=0, pattern=[[-STATES, GD]], channel_multiplier=1).then_inc(consts, 1)
            pool.wait_ge(consts, 6)
            pool.affine_select(out=own[:, :], in_=own[:, :], compare_op=ALU.is_ge, fill=0.0,
                               base=STATES - 1, pattern=[[STATES, GD]], channel_multiplier=-1).then_inc(consts, 1)
            for e in range(EXPERTS):
                pool.memset(iota8[:, :, e:e + 1], float(e)).then_inc(consts, 1)

            def inverse_root(k, have, n, src, scale, mid, mid_sem, dst, dst_sem):
                pool.wait_ge(have, n)
                pool.tensor_scalar(mid[:, :], src, scale, EPS, ALU.mult, ALU.add).then_inc(mid_sem, 1)
                pool.wait_ge(mid_sem, k + 1)
                pool.tensor_tensor(dst[:, :], mid[:, :], mhalf[:, :], ALU.pow).then_inc(dst_sem, 1)

            def ln_root(k):
                inverse_root(k, ln_mv, k + 1, mv[:, :, 1], 1.0, ve, ln_ve, rstd, ln_rstd)

            def rms_root(k):
                inverse_root(k, rms_ms, k + 1, ms[:, :], 1.0 / D, me, rms_me, rr, rms_r)

            def softplus_sum(k):
                pool.wait_ge(l_done, k + 1)
                pool.wait_ge(corr_done, k + 1)
                pool.tensor_tensor(lg1p[:, :, :], lg1p[:, :, :], corr[:, :, :], ALU.subtract).then_inc(lsum_done, 1)
                pool.wait_ge(lsum_done, k + 1)
                if k > 0:
                    for b in range(DB):
                        pool.wait_ge(stacked[b], 16 * 3 * NQ * k)
                pool.tensor_tensor(parts[:, :, 0, 0, :], lg1p[:, :, :], rl[:, :, :], ALU.add).then_inc(dt_done, 1)

            def times_C(c, n):
                u = UNITS * c + n
                pool.wait_ge(scan_done, u + 1)
                if u >= 2 * PACK:
                    pool.wait_ge(reduced, u // PACK - 1)
                pool.tensor_tensor(hc[:, n % (2 * PACK), :], hs[:, u % 3, :], Ct[:, c % 2, :], ALU.mult)\
                    .then_inc(hc_done, 1)

            def finish(c):
                pool.wait_ge(g_done, c + 1)
                wait_emptied(pool, c, "o")
                pool.tensor_tensor(s_sb[:, c, :], s_sb[:, c, :], acc[:, c, :], ALU.mult).then_inc(sg_done, 1)
                pool.wait_ge(sg_done, c + 1)
                pool.tensor_tensor(s_sb[:, c, :], s_sb[:, c, :],
                                   x_sb[:, c].rearrange("p t d -> p (t d)"), ALU.add).then_inc(o_done, 1)

            ln_root(0)
            rms_root(0)
            softplus_sum(0)
            for c in range(CHUNKS):
                for n in range(UNITS):
                    times_C(c, n)
                    if c < CHUNKS - 1:
                        if n == 0:
                            ln_root(c + 1)
                        if n == 1:
                            rms_root(c + 1)
                        if n == 17:
                            softplus_sum(c + 1)
                    elif n in (12, 16, 20):
                        finish((n - 12) // 4)
            finish(CHUNKS - 1)

        @block.scalar
        def _(act):
            act.preload_act_table_set("natural_log_exp_and_others")
            act.wait_ge(vec_t, 1)
            act.activation(cols[:, :], px[0][:, 0:V_END], ACT.Copy).then_inc(vec_c, 1)
            act.wait_ge(vec_c, 1)
            act.activation(negA[:, :], cols[:, V_A:V_A + 32], ACT.Exp).then_inc(expA, 1)

            def squares(k):
                act.wait_ge(ln_xn, k + 1)
                if k > 0:
                    act.wait_ge(rms_ms, k)
                    act.wait_ge(rms_me, k)
                for i in range(TPC):
                    last = act.activation(sq[:, i, :], xn[:, k, i, :], ACT.Square, accum_out=ms[:, i:i + 1])
                last.then_inc(rms_ms, 1)

            def decay(c, n):
                u = UNITS * c + n
                b, gl, q = n // (GL * NQ), n // NQ % GL, n % NQ
                g = (b * NQ + q) * GL + gl
                act.wait_ge(dt_spread, u + 1)
                act.activation(pd[n % 2][:, :], pd[n % 2][:, :], ACT.Exp, scale=negA[:, g:g + 1]).then_inc(decay_done, 1)

            def silu(k):
                act.preload_act_table_set("silu_and_others")
                wait_emptied(act, k - 1, "xc1")
                if k >= 2:
                    act.wait_ge(yg_done, DB * (k - 1))
                act.activation(xc[:, k % 2], xv[:, :, :], ACT.Silu).then_inc(silu_done, 1)
                act.activation(sz[:, k % 2], zr[:, :, :], ACT.Silu).then_inc(silu_done, 1)
                act.preload_act_table_set("natural_log_exp_and_others")

            def log1p_exp(k):
                wait_emptied(act, k - 1, "v1")
                act.activation(ev[:, :, :], ev[:, :, :], ACT.Exp, scale=-1.0).then_inc(e_done, 1)
                act.wait_ge(e_done, k + 1)
                act.activation(lg1p[:, :, :], ev[:, :, :], ACT.Ln, bias=1.0).then_inc(l_done, 1)

            def empty(c, job):
                if job in EMPTIED_BY_DVE:
                    return
                k = c + 1
                src = bank_of(c, job)
                j = base(c)[0] + jobs_of(c).index(job)
                wait_filled(act, c, job)
                if job == "tn":
                    if c >= 0:
                        wait_emptied(act, c - 1, "gl")
                        act.wait_ge(xnT_copied, c + 1)
                    ins = act.activation(xnT_next[:, :], src[:, :], ACT.Copy)
                elif job == "tr":
                    ins = act.activation(xrT[:, :, PAD:PAD + SEQ], src[:, :].rearrange("p (b t) -> p b t", b=BPC),
                                         ACT.Copy, scale=cols[:, V_NW:V_NW + 1])
                elif job in ("z0", "z1"):
                    if k > 0:
                        act.wait_ge(dt_done, k)
                    ins = act.activation(zr[:, int(job[1]), :], src[:, :], ACT.Copy)
                elif job in ("xc0", "xc1"):
                    b = int(job[2])
                    if k > 0:
                        act.wait_ge(lsum_done, k)
                    ins = act.activation(xv[:, b, :], src[:, :], ACT.Identity, bias=cols[:, V_CB + b:V_CB + b + 1])
                elif job == "dt":
                    ins = act.activation(dtp[:, :], src[:, :], ACT.Copy)
                elif job == "B":
                    if k >= 2:
                        act.wait_ge(dbu_done, UNITS * (k - 1))
                    ins = act.activation(Bt[:, k % 2, :], src[:, :], ACT.Copy)
                elif job == "C":
                    if k >= 2:
                        act.wait_ge(hc_done, UNITS * (k - 1))
                    ins = act.activation(Ct[:, k % 2, :], src[:, :], ACT.Copy)
                elif job in ("v0", "v1"):
                    b = int(job[1])
                    if k > 0:
                        act.wait_ge(corr_done, k)
                        act.wait_ge(dt_done, k)
                    act.activation(rl[:, b, :], src[:, :], ACT.Relu, bias=cols[:, V_BDT + b:V_BDT + b + 1])
                    ins = act.activation(ev[:, b, :], src[:, :], ACT.Abs, bias=cols[:, V_BDT + b:V_BDT + b + 1])
                elif job == "gs":
                    ins = act.activation(sT[:, :], src[0:TPC * EXPERTS, 0:P], ACT.Copy)
                elif job == "gb":
                    ins = act.activation(acc[:, k, :], src[:, :], ACT.Copy)
                elif job[0] == "m":
                    e, b = int(job[1]), "ab".index(job[2])
                    if e >= 2:
                        act.wait_ge(filled, base(c)[0] + jobs_of(c).index(f"y{e - 2}") + 1)
                    elif c > 0:
                        act.wait_ge(filled, base(c - 1)[0] + jobs_of(c - 1).index(f"y{e + 6}") + 1)
                    ins = act.activation(hT[:, e % 2, b, :], src[:, :], ACT.Relu,
                                         bias=cols[:, V_B1 + HB * e + b:V_B1 + HB * e + b + 1])
                else:
                    ins = act.activation(nops[:, j:j + 1], src[:, 0:1], ACT.Copy)
                ins.then_inc(act_emptied, 1)

            def gate_e(k):
                act.wait_ge(gate_step, GATE_STEPS * k + 2)
                act.activation(gex[:, :, :], glc[:, :, :], ACT.Exp).then_inc(gate_exp, 1)

            def copy_xnT(c):
                wait_emptied(act, c - 1, "tn")
                if c > 0:
                    wait_emptied(act, c - 1, "m7b")
                act.activation(xnT[:, :], xnT_next[:, :], ACT.Copy).then_inc(xnT_copied, 1)

            squares(0)
            for job in PRE_JOBS:
                if job == "dt":
                    silu(0)
                if job == "gs":
                    gate_e(0)
                empty(-1, job)
            log1p_exp(0)
            copy_xnT(0)
            decay(0, 0)
            for c in range(CHUNKS):
                more = c < CHUNKS - 1
                if c > 0:
                    copy_xnT(c)
                for n in range(UNITS):
                    if n + 1 < UNITS:
                        decay(c, n + 1)
                    elif more:
                        decay(c + 1, 0)
                    if more and n == 1:
                        squares(c + 1)
                    if more and n == 10:
                        silu(c + 1)
                    if more and n == 9:
                        gate_e(c + 1)
                    for job in SLOTS[n]:
                        if job in jobs_of(c):
                            empty(c, job)
                    if more and n == 15:
                        log1p_exp(c + 1)
                    if not more and n == 10:
                        act.preload_act_table_set("silu_and_others")
                        for k in range(CHUNKS - 1):
                            act.wait_ge(moe_acc, EXPERTS * TPC * (k + 1))
                            act.activation(acc[:, k, :], acc[:, k, :], ACT.Silu).then_inc(g_done, 1)
                        act.preload_act_table_set("natural_log_exp_and_others")
            act.preload_act_table_set("silu_and_others")
            act.wait_ge(moe_acc, EXPERTS * TPC * CHUNKS)
            act.activation(acc[:, CHUNKS - 1, :], acc[:, CHUNKS - 1, :], ACT.Silu).then_inc(g_done, 1)

        @block.vector
        def _(dve):
            dve.memset(xrT[:, :, 0:PAD], 0.0).then_inc(setup, 1)
            dve.memset(wR[:, :, :], 0.0).then_inc(setup, 1)
            dve.memset(wdt[RANK:P, :], 0.0).then_inc(setup, 1)
            dve.memset(rsel[:, :, :], 0.0).then_inc(setup, 1)

            def stats(k):
                dve.wait_ge(x_first if k == 0 else x_rest, 16)
                for i in range(TPC):
                    last = dve.bn_stats(st[:, i, :], x_sb[:, k, i, :])
                last.then_inc(ln_st, 1)
                dve.wait_ge(ln_st, k + 1)
                if k > 0:
                    dve.wait_ge(ln_ve, k)
                for i in range(TPC):
                    last = dve.bn_aggr(mv[:, i, :], st[:, i, :])
                last.then_inc(ln_mv, 1)

            def normalise(k):
                dve.wait_ge(ln_mv, k + 1)
                dve.wait_ge(ln_rstd, k + 1)
                for i in range(TPC):
                    last = dve.tensor_scalar(xn[:, k, i, :], x_sb[:, k, i, :], mv[:, i, 0:1], rstd[:, i:i + 1],
                                             ALU.subtract, ALU.mult)
                last.then_inc(ln_xn, 1)

            def scale_rows(k):
                dve.wait_ge(ln_xn, k + 1)
                dve.wait_ge(rms_r, k + 1)
                if k > 0:
                    wait_emptied(dve, k - 2, "tr")
                for i in range(TPC):
                    last = dve.tensor_scalar(xr[:, i, :], xn[:, k, i, :], rr[:, i:i + 1], None, ALU.mult)
                last.then_inc(rms_xr, 1)

            stats(0)
            normalise(0)
            dve.wait_ge(w_in, 16 * N_WIN)
            for t in range(TAPS):
                dve.tensor_tensor(wtap[:, t, :], win[:, 0:DIN], cwb[:, :, t], ALU.mult).then_inc(setup, 1)
            scale_rows(0)
            dve.wait_ge(setup, 8)
            for b in range(DB):
                for w, o in ((wB, RANK), (wC, RANK + STATES)):
                    dve.tensor_copy(w[:, b], wx[:, b, None, o:o + STATES].to_broadcast([P, GD, STATES])).then_inc(setup, 1)
                dve.tensor_copy(wR[:, b, 0:RANK], wx[:, b, 0:RANK]).then_inc(setup, 1)
            dve.wait_ge(consts, 7)
            for p in range(3):
                s = slice(32 * p, 32 * p + 32)
                dve.tensor_copy(sel[s, :, :, :].rearrange("p g d s -> p (g d) s"),
                                ident[s, s, None].to_broadcast([32, 32, STATES])).then_inc(setup, 1)
            for g in range(GL):
                dve.tensor_copy(rsel[:, g, g * GD:(g + 1) * GD], own[:, :]).then_inc(setup, 1)
            dve.wait_ge(expA, 1)
            dve.tensor_scalar(negA[:, :], negA[:, :], -1.0, None, ALU.mult).then_inc(setup, 1)

            def gate(k):
                n = [GATE_STEPS * k]

                def link(ins):
                    n[0] += 1
                    ins.then_inc(gate_step, 1)
                    dve.wait_ge(gate_step, n[0])

                src = bank_of(k - 1, "gl")[:, 0:TPC * EXPERTS].rearrange("p (t e) -> p t e", e=EXPERTS)
                wide = [P, TPC, EXPERTS]
                wait_filled(dve, k - 1, "gl")
                link(dve.tensor_reduce(gmx[:, :], src, AX.X, ALU.max))
                dve.tensor_tensor(glc[:, :, :], src, gmx[:, :, None].to_broadcast(wide), ALU.subtract).then_inc(gate_step, 1)
                n[0] += 1
                dve.wait_ge(gate_step, n[0])
                dve.tensor_copy(gs2[:, 0:1], src[:, 0, 0:1]).then_inc(dve_emptied, 1)
                yield
                dve.wait_ge(gate_exp, k + 1)
                link(dve.tensor_reduce(gsm[:, :], gex[:, :, :], AX.X, ALU.add))
                link(dve.reciprocal(gri[:, :], gsm[:, :]))
                link(dve.tensor_tensor(gp[:, :, :], gex[:, :, :], gri[:, :, None].to_broadcast(wide), ALU.mult))
                for i in range(TPC):
                    last = dve.max(gv8[:, i, :], gp[:, i, :])
                link(last)
                for i in range(TPC):
                    last = dve.max_index(gi8[:, i, :], gv8[:, i, :], gp[:, i, :])
                link(last)
                yield
                link(dve.tensor_copy(gif[:, :, :], gi8[:, :, 0:2]))
                link(dve.tensor_tensor(gs2[:, :], gv8[:, :, 0], gv8[:, :, 1], ALU.add))
                link(dve.reciprocal(grs[:, :], gs2[:, :]))
                link(dve.tensor_tensor(gvn[:, :, :], gv8[:, :, 0:2], grs[:, :, None].to_broadcast([P, TPC, 2]), ALU.mult))
                for j in range(2):
                    last = dve.tensor_tensor(goh[:, j], iota8[:, :, :], gif[:, :, j:j + 1].to_broadcast(wide), ALU.is_equal)
                link(last)
                for j in range(2):
                    last = dve.tensor_tensor(gw[:, j], goh[:, j], gvn[:, :, j:j + 1].to_broadcast(wide), ALU.mult)
                link(last)
                link(dve.tensor_tensor(score[:, k % 2], gw[:, 0], gw[:, 1], ALU.add))
                assert n[0] == GATE_STEPS * (k + 1), n[0]
                yield

            def correction(k):
                dve.wait_ge(e_done, k + 1)
                dve.tensor_scalar(corr[:, :, :], ev[:, :, :], 1.0, -1.0, ALU.add, ALU.add).then_inc(round_done, 1)
                dve.wait_ge(round_done, k + 1)
                dve.tensor_tensor(corr[:, :, :], corr[:, :, :], ev[:, :, :], ALU.subtract).then_inc(corr_done, 1)

            def upper(t):
                return t.bitcast(BF16).rearrange("p a b (t two) -> p a b t two", two=2)[:, :, :, :, 1]

            def times_dt(k):
                dve.wait_ge(dt_done, k + 1)
                dve.tensor_tensor(parts[:, :, 1, 0, :], parts[:, :, 0, 0, :], xc[:, k % 2], ALU.mult).then_inc(u_done, 1)
                dve.wait_ge(u_done, k + 1)
                dve.memset(parts[:, :, 0, 0, SEQ:CH:SEQ], FAR).then_inc(far_done, 1)
                dve.wait_ge(far_done, k + 1)

            def split(k, b, first):
                p = 0 if first else 1
                if not first:
                    dve.wait_ge(r1_done, DB * k + b + 1)
                src = parts[:, b, :, p, :]
                up = src.bitcast(BF16).rearrange("p a (t two) -> p a t two", two=2)[:, :, :, 1]
                ins = dve.tensor_tensor(parts[:, b, :, p + 1, :], src, up, ALU.subtract)
                if first:
                    ins.then_inc(r1_done, 1)
                elif b == DB - 1:
                    ins.then_inc(parts_done, 1)

            def times_B(c, n):
                u = UNITS * c + n
                dve.wait_ge(u_spread, u + 1)
                if u >= 2:
                    dve.wait_ge(scan_done, u - 1)
                dve.tensor_tensor(dbu[:, n % 2, :], pu[n % 2][:, :], Bt[:, c % 2, :], ALU.mult).then_inc(dbu_done, 1)

            def scan(c, n):
                u = UNITS * c + n
                dve.wait_ge(decay_done, u + 1)
                dve.wait_ge(dbu_done, u + 1)
                if u >= 3:
                    dve.wait_ge(hc_done, u - 2)
                dve.tensor_tensor_scan(hs[:, u % 3, :], pd[n % 2][:, :], dbu[:, n % 2, :], 0.0, ALU.mult, ALU.add)\
                    .then_inc(scan_done, 1)

            def gate_y(c, b):
                i = DB * c + b
                dve.wait_ge(reduced, UNITS // PACK * c + (b + 1) * UNITS // PACK // DB)
                if c > 0:
                    wait_emptied(dve, c - 1, "o")
                dve.scalar_tensor_tensor(yg[:, b, :], xc[:, c % 2, b, :], cols[:, V_DS + b:V_DS + b + 1], py[:, :],
                                         ALU.mult, ALU.add).then_inc(y_taken, 1)
                dve.wait_ge(y_taken, i + 1)
                dve.tensor_tensor(yg[:, b, :], yg[:, b, :], sz[:, c % 2, b, :], ALU.mult).then_inc(yg_done, 1)

            def empty(c, job):
                if job[0] == "y":
                    e = int(job[1])
                    src = bank_of(c, job)
                    wait_filled(dve, c, job)
                    if e == 0:
                        wait_emptied(dve, c - 1, "gb")
                    for i in range(TPC):
                        t = slice(i * D, (i + 1) * D)
                        n = (c * EXPERTS + e) * TPC + i
                        if e > 0:
                            dve.wait_ge(moe_acc, n - TPC + 1)
                        dve.scalar_tensor_tensor(acc[:, c, t], src[:, t], score[:, c % 2, i, e:e + 1], acc[:, c, t],
                                                 ALU.mult, ALU.add).then_inc(moe_acc, 1)
                    dve.wait_ge(moe_acc, (c * EXPERTS + e + 1) * TPC)
                    dve.tensor_copy(gs2[:, 0:1], src[:, 0:1]).then_inc(dve_emptied, 1)
                elif job == "o":
                    wait_filled(dve, c, job)
                    dve.tensor_tensor(s_sb[:, c, :], bank_of(c, job)[:, :], xn[:, c].rearrange("p t d -> p (t d)"),
                                      ALU.add).then_inc(dve_emptied, 1)

            for _ in gate(0):
                pass
            correction(0)
            times_dt(0)
            for b in range(DB):
                split(0, b, True)
            for b in range(DB):
                split(0, b, False)
            times_B(0, 0)
            for c in range(CHUNKS):
                more = c < CHUNKS - 1
                gates = gate(c + 1) if more else None
                for n in range(UNITS):
                    if n + 1 < UNITS:
                        times_B(c, n + 1)
                    elif more:
                        times_B(c + 1, 0)
                    scan(c, n)
                    if n == 18:
                        gate_y(c, 0)
                    if more:
                        if n == 0:
                            stats(c + 1)
                            normalise(c + 1)
                        if n == 1:
                            scale_rows(c + 1)
                        if n in (7, 9, 10):
                            next(gates)
                        if n == 15:
                            correction(c + 1)
                        if n == 18:
                            times_dt(c + 1)
                        if n in (19, 20):
                            split(c + 1, n - 19, True)
                        if n in (21, 22):
                            split(c + 1, n - 21, False)
                    for job in SLOTS[n]:
                        if job in jobs_of(c) and job in EMPTIED_BY_DVE:
                            empty(c, job)
                gate_y(c, 1)
                empty(c, "o")

        @block.tensor
        def _(pe):
            pe.wait_ge(w_in, 16 * N_WIN)
            pe.wait_ge(consts, 7)
            pe.transpose(px[0][:, 0:V_END], rows[:, :], ident[0:V_END, 0:V_END]).then_inc(vec_t, 1)

            def spread(c, n):
                u = UNITS * c + n
                b, gl, q = n // (GL * NQ), n // NQ % GL, n % NQ
                if n % (GL * NQ) == 0:
                    pe.wait_ge(stacked[b], 16 * 3 * NQ * (c + 1))
                w = sel[:, gl].rearrange("p d s -> p (d s)")
                for kind, dst, used, done in ((0, pd, scan_done, dt_spread), (1, pu, dbu_done, u_spread)):
                    if u >= 2:
                        pe.wait_ge(used, u - 1)
                    up = stack[0:96, b, q, kind, :].bitcast(BF16).rearrange("p (t two) -> p t two", two=2)[:, :, 1]
                    pe.matmul(dst[n % 2][:, :], w, up, start=True, stop=True).then_inc(done, 1)

            def reduce_pack(c, m):
                b, gl = m // GL, m % GL
                pe.wait_ge(hc_done, UNITS * c + PACK * (m + 1))
                if gl == 0 and DB * c + b > 0:
                    pe.wait_ge(y_taken, DB * c + b)
                for q in range(NQ):
                    last = pe.matmul(py[32 * q:32 * q + 32, :], rsel[:, gl, :], hc[:, (PACK * m + q) % (2 * PACK), :],
                                     start=gl == 0, stop=gl == GL - 1)
                last.then_inc(reduced, 1)

            def fill(c, job):
                jobs, k = jobs_of(c), c + 1
                j = jobs.index(job)
                dst = px[j % AUX]
                if j >= AUX:
                    wait_emptied(pe, c, jobs[j - AUX])
                elif c >= 0:
                    pe.wait_ge(act_emptied, base(c)[1])
                    pe.wait_ge(dve_emptied, base(c)[2])
                elif j == 0:
                    pe.wait_ge(vec_c, 1)
                if job == "tn":
                    pe.wait_ge(ln_xn, k + 1)
                    for i in range(TPC):
                        last = pe.transpose(dst[:, i * P:(i + 1) * P], xn[:, k, i, :], ident[:, :])
                elif job == "tr":
                    pe.wait_ge(rms_xr, k + 1)
                    for i in range(TPC):
                        last = pe.transpose(dst[:, i * P:(i + 1) * P], xr[:, i, :], ident[:, :])
                elif job in ("z0", "z1"):
                    wait_emptied(pe, c, "tr")
                    o = DIN + int(job[1]) * P
                    last = pe.matmul(dst[:, :], win[:, o:o + P], xrT[:, :, PAD:PAD + SEQ], start=True, stop=True)
                elif job in ("xc0", "xc1"):
                    wait_emptied(pe, c, "tr")
                    if c < 0:
                        pe.wait_ge(setup, 8)
                    b = int(job[2])
                    for t in range(TAPS):
                        last = pe.matmul(dst[:, :], wtap[:, t, b * P:(b + 1) * P], xrT[:, :, t:t + SEQ],
                                         start=t == 0, stop=t == TAPS - 1)
                elif job in ("dt", "B", "C"):
                    pe.wait_ge(silu_done, 2 * k + 1)
                    if c < 0:
                        pe.wait_ge(setup, 14)
                    for b in range(DB):
                        w = {"dt": wR[:, b, :], "B": wB[:, b].rearrange("p d s -> p (d s)"),
                             "C": wC[:, b].rearrange("p d s -> p (d s)")}[job]
                        last = pe.matmul(dst[:, :], w, xc[:, k % 2, b, :], start=b == 0, stop=b == DB - 1)
                elif job in ("v0", "v1"):
                    wait_emptied(pe, c, "dt")
                    b = int(job[1])
                    last = pe.matmul(dst[:, :], wdt[:, b * P:(b + 1) * P], dtp[:, :], start=True, stop=True)
                elif job == "gl":
                    wait_emptied(pe, c, "tn")
                    for i in range(TPC):
                        last = pe.matmul(dst[:, i * EXPERTS:(i + 1) * EXPERTS], xnT_next[:, i * P:(i + 1) * P], wg[:, :],
                                         start=True, stop=True)
                elif job == "gs":
                    pe.wait_ge(gate_step, GATE_STEPS * (k + 1))
                    last = pe.transpose(dst[0:TPC * EXPERTS, 0:P], score[:, k % 2].rearrange("p t e -> p (t e)"), ident[:, :])
                elif job == "gb":
                    wait_emptied(pe, c, "gs")
                    if c < 0:
                        pe.wait_ge(w_moe, 16 * 6)
                    last = pe.matmul(dst[:, :], sT[:, :], b2d[:, :, :].rearrange("e t d -> e (t d)"), start=True, stop=True)
                elif job[0] == "m":
                    e, b = int(job[1]), "ab".index(job[2])
                    pe.wait_ge(xnT_copied, c + 1)
                    last = pe.matmul(dst[:, :], w1[:, e, b * P:(b + 1) * P], xnT[:, :], start=True, stop=True)
                elif job[0] == "y":
                    e = int(job[1])
                    wait_emptied(pe, c, f"m{e}b")
                    for i in range(TPC):
                        for b in range(HB):
                            last = pe.matmul(dst[:, i * D:(i + 1) * D], hT[:, e % 2, b, i * P:(i + 1) * P], w2[:, e, b, :],
                                             start=b == 0, stop=b == HB - 1)
                elif job == "o":
                    pe.wait_ge(yg_done, DB * (c + 1))
                    for i in range(TPC):
                        for b in range(DB):
                            last = pe.matmul(dst[:, i * D:(i + 1) * D], yg[:, b, i * P:(i + 1) * P], wout[:, b, :],
                                             start=b == 0, stop=b == DB - 1)
                else:
                    last = pe.matmul(dst[:, 0:EXPERTS], ident[:, :], wg[:, :], start=True, stop=True)
                last.then_inc(filled, 1)

            for job in PRE_JOBS:
                fill(-1, job)
            pe.wait_ge(setup, 22)
            spread(0, 0)
            for c in range(CHUNKS):
                for n in range(UNITS):
                    if n + 1 < UNITS:
                        spread(c, n + 1)
                    elif c < CHUNKS - 1:
                        spread(c + 1, 0)
                    for job in SLOTS[n]:
                        if job in jobs_of(c):
                            fill(c, job)
                    if n in REDUCE_AT:
                        reduce_pack(c, REDUCE_AT[n])
                reduce_pack(c, UNITS // PACK - 1)
                fill(c, "o")


_INS = ["L0_attn_x", "L0_attn_norm_w", "L0_attn_W_in", "L0_attn_conv_w", "L0_attn_conv_b", "L0_attn_W_x",
        "L0_attn_W_dt", "L0_attn_b_dt", "L0_attn_A_log", "L0_attn_D_skip", "L0_attn_W_out",
        "L0_ffn_Wg", "L0_ffn_W1", "L0_ffn_b1", "L0_ffn_W2", "L0_ffn_b2"]


def kernel(**inputs):
    import numpy as np
    import concourse.bacc as bacc
    from concourse.bass_utils import run_bass_kernel_spmd

    nc = bacc.Bacc("TRN2", target_bir_lowering=False, num_devices=1)
    arrays, args = {}, []
    for name in _INS:
        a = np.ascontiguousarray(inputs[name])
        arrays[f"in_{name}"] = a
        args.append(nc.dram_tensor(f"in_{name}", a.shape, mybir.dt.from_np(a.dtype), kind="ExternalInput").ap())
    args.append(nc.dram_tensor("out_0", (BATCH, SEQ, D), F32, kind="ExternalOutput").ap())
    mamba_moe(nc, *args)
    r = run_bass_kernel_spmd(nc, [arrays], core_ids=[0])
    return r.results[0]["out_0"]
```

```python
from contextlib import ExitStack

import concourse.bass as bass
from concourse import mybir

ALU = mybir.AluOpType
ACT = mybir.ActivationFunctionType
AX = mybir.AxisListType
F32 = mybir.dt.float32
BF16 = mybir.dt.bfloat16
U32 = mybir.dt.uint32

P = 128
BATCH, SEQ, D = 8, 256, 128
DIN, STATES, RANK, TAPS = 256, 16, 64, 4
EXPERTS, HID = 8, 256
EPS = 1e-5
TOK = BATCH * SEQ
CH = 512
BPC = CH // SEQ
TPC = CH // P
CHUNKS = TOK // CH
TILES = TOK // P
NORM = [range(0, TPC), range(TPC, TILES)]
DB = DIN // P
GD = P // STATES
GL = 32 // GD
NQ = P // 32
UNITS = DB * GL * NQ
PACK = NQ
HB = HID // P
PAD = TAPS - 1
FAR = 1.0e28

V_A, V_B1, V_BDT, V_CB, V_DS, V_NW, V_END = 0, 32, 48, 50, 52, 54, 55

PRE_JOBS = ["tn", "tr", "xc0", "z0", "xc1", "z1", "gl", "dt", "v0", "v1", "B", "C", "gs", "gb", "nop"]
EMPTIED_BY_DVE = {"gl", "o"} | {f"y{e}" for e in range(EXPERTS)}
HEAD = 5
SLOTS = {
    5: ["tr"], 6: ["xc0<"], 7: ["xc0"], 8: ["xc1<"], 9: ["m0a"], 10: ["xc1"], 11: ["z0", "z1"],
    12: ["m0b", "m1a"], 13: ["m1b"], 14: ["dt"], 15: ["v0", "v1"], 16: ["y0"], 17: ["tn"],
    18: ["gl", "m2a"], 19: ["y1"], 20: ["m2b", "m3a"], 21: ["m3b"], 22: ["y2"], 23: ["B", "gs"],
    24: ["C"], 25: ["m4a"], 26: ["gb"], 27: ["y3"], 28: ["m4b", "m5a"], 29: ["m5b"], 30: ["y4"],
    31: ["y5", "m6a"], 32: ["m6b", "m7a"], 33: ["m7b"], 34: ["y6"], 35: ["y7"], 36: ["o"],
}
PERIOD_JOBS = [j for n in sorted(SLOTS) for j in SLOTS[n] if j[-1] != "<"]
GATE_STEPS = 13
STARTED = {j for n in SLOTS for j in SLOTS[n] if j[-1] == "<"}
AUX = 3
LAG = 2
SUM_Y = [UNITS // DB + LAG, UNITS + LAG]


def emptied(jobs, name=None):
    upto = jobs if name is None else jobs[:jobs.index(name) + 1]
    v = sum(j in EMPTIED_BY_DVE for j in upto)
    return len(upto) - v, v


def mamba_moe(nc, x, norm_w, W_in, conv_w, conv_b, W_x, W_dt, b_dt, A_log, D_skip, W_out,
              Wg, W1, b1, W2, b2, out):
    last_jobs = [j for j in PERIOD_JOBS if j not in PRE_JOBS and j[:3] != "nop"]
    assert len(PRE_JOBS) % AUX == 0 and len(PERIOD_JOBS) % AUX == 0, (len(PRE_JOBS), len(PERIOD_JOBS))

    with ExitStack() as ctx:
        def sb(name, shape, dt=F32):
            return ctx.enter_context(nc.sbuf_tensor(name, shape, dt))

        def sem(name):
            return ctx.enter_context(nc.semaphore(name))

        x_sb = sb("x_sb", [P, CHUNKS, TPC, D])
        xn = sb("xn", [P, CHUNKS, TPC, D])
        acc = sb("acc", [P, CHUNKS, CH])
        s_sb = xn[:, :, :, :].rearrange("p c t d -> p c (t d)")
        xr = sb("xr", [P, TPC, D])
        sq = sb("sq", [P, 2, D])
        xnT_next = sb("xnT_next", [P, CH])
        xnT = sb("xnT", [P, CH])
        xrT = sb("xrT", [P, BPC, PAD + SEQ])
        zr = sb("zr", [P, DB, CH])
        xv = sb("xv", [P, DB, CH])
        sz = sb("sz", [P, 2, DB, CH])
        xc = sb("xc", [P, 2, DB, CH])
        Bt = sb("Bt", [P, 2, CH])
        Ct = sb("Ct", [P, 2, CH])
        dtp = sb("dtp", [P, CH])
        ev = sb("ev", [P, DB, CH])
        rl = sb("rl", [P, DB, CH])
        lg1p, corr = zr, xv
        parts = sb("parts", [P, DB, 2, 3, CH])
        stack = sb("stack", [P, DB, NQ, 2, CH])
        win = sb("win", [P, 2 * DIN])
        wtap = sb("wtap", [P, TAPS, DIN])
        cwb = parts[:, 0, 0, 0:2, :].rearrange("p a b -> p (a b)").rearrange("p (d k) -> p d k", k=TAPS)
        wx = sb("wx", [P, DB, RANK + 2 * STATES])
        wB = sb("wB", [P, DB, GD, STATES])
        wC = sb("wC", [P, DB, GD, STATES])
        wR = sb("wR", [P, DB, P])
        wdt = sb("wdt", [P, DIN])
        wout = sb("wout", [P, DB, D])
        wg = sb("wg", [P, EXPERTS])
        w1 = sb("w1", [P, EXPERTS, HID])
        w2 = sb("w2", [P, EXPERTS, HB, D])
        b2d = sb("b2d", [TPC * EXPERTS, TPC, D])
        rows = sb("rows", [V_END, P])
        cols = sb("cols", [P, V_END])
        negA = sb("negA", [P, 32])
        ident = sb("ident", [P, P])
        own = sb("own", [P, GD])
        sel = sb("sel", [96, GL, GD, STATES], BF16)
        rsel = sb("rsel", [P, GL, 32])
        iota8 = sb("iota8", [P, TPC, EXPERTS])
        mhalf = sb("mhalf", [P, TILES])
        st = sb("st", [P, TILES, 6])
        mv = sb("mv", [P, TILES, 2])
        nops = sb("nops", [P, len(PRE_JOBS) + CHUNKS * len(PERIOD_JOBS)])
        ve = sb("ve", [P, TILES])
        rstd = sb("rstd", [P, TILES])
        ms = sb("ms", [P, TILES])
        me = sb("me", [P, TILES])
        rr = sb("rr", [P, TILES])
        gmx = sb("gmx", [P, TPC])
        glc = sb("glc", [P, TPC, EXPERTS])
        gex = sb("gex", [P, TPC, EXPERTS])
        gsm = sb("gsm", [P, TPC])
        gri = sb("gri", [P, TPC])
        gp = sb("gp", [P, TPC, EXPERTS])
        gv8 = sb("gv8", [P, TPC, 8])
        gi8 = sb("gi8", [P, TPC, 8], U32)
        gif = sb("gif", [P, TPC, 2])
        gs2 = sb("gs2", [P, TPC])
        grs = sb("grs", [P, TPC])
        gvn = sb("gvn", [P, TPC, 2])
        goh = sb("goh", [P, 2, TPC, EXPERTS])
        gw = sb("gw", [P, 2, TPC, EXPERTS])
        score = sb("score", [P, 2, TPC, EXPERTS])
        sT = sb("sT", [TPC * EXPERTS, P])
        dbu = sb("dbu", [P, 2, CH])
        hs = sb("hs", [P, 3, CH])
        hc = sb("hc", [P, 2 * PACK, CH])
        hT = sb("hT", [P, 2, HB, CH])
        yg = sb("yg", [P, DB, CH])

        def bank(name):
            return ctx.enter_context(nc.psum_tensor(name, [P, CH], F32))

        pd = [bank(f"pd{i}") for i in range(2)]
        pu = [bank(f"pu{i}") for i in range(2)]
        py = bank("py")
        px = [bank(f"px{i}") for i in range(AUX)]

        x_first, x_rest = sem("x_first"), sem("x_rest")
        w_in, w_moe = sem("w_in"), sem("w_moe")
        consts = sem("consts")
        setup = sem("setup")
        vec_t, vec_c, expA = sem("vec_t"), sem("vec_c"), sem("expA")
        ln_mv, ln_ve, ln_rstd, ln_xn = sem("ln_mv"), sem("ln_ve"), sem("ln_rstd"), sem("ln_xn")
        ln_st = sem("ln_st")
        rms_sq, rms_me, rms_r, rms_xr = sem("rms_sq"), sem("rms_me"), sem("rms_r"), sem("rms_xr")
        silu_done = sem("silu_done")
        e_done, l_done = sem("e_done"), sem("l_done")
        round_done, corr_done, lsum_done, dt_done = sem("round_done"), sem("corr_done"), sem("lsum_done"), sem("dt_done")
        u_done, far_done, r1_done, r2_done = sem("u_done"), sem("far_done"), sem("r1_done"), sem("r2_done")
        stacked = [sem("stacked0"), sem("stacked1")]
        gate_exp, gate_step, score_done = sem("gate_exp"), sem("gate_step"), sem("score_done")
        xnT_copied = sem("xnT_copied")
        filled = sem("filled")
        act_emptied, dve_emptied = sem("act_emptied"), sem("dve_emptied")
        dt_spread, u_spread = sem("dt_spread"), sem("u_spread")
        decay_done, dbu_done, scan_done, hc_done = sem("decay_done"), sem("dbu_done"), sem("scan_done"), sem("hc_done")
        reduced = sem("reduced")
        y_taken, yg_done = sem("y_taken"), sem("yg_done")
        g_done, sg_done, o_done, stored = sem("g_done"), sem("sg_done"), sem("o_done"), sem("stored")

        xv_dram = x.rearrange("b (h p) d -> p (b h) d", p=P)
        ov_dram = out.rearrange("b (h p) d -> p (b h) d", p=P)
        N_WIN, N_WMOE = 12, 3

        PA, PV = emptied(PRE_JOBS)
        QA, QV = emptied(PERIOD_JOBS)
        NPRE, NPER = len(PRE_JOBS), len(PERIOD_JOBS)

        def base(c):
            return (0, 0, 0) if c < 0 else (NPRE + c * NPER, PA + c * QA, PV + c * QV)

        def jobs_of(c):
            return PRE_JOBS if c < 0 else (PERIOD_JOBS if c < CHUNKS - 1 else last_jobs)

        def bank_of(c, job):
            return px[jobs_of(c).index(job) % AUX]

        def wait_filled(eng, c, job):
            eng.wait_ge(filled, base(c)[0] + jobs_of(c).index(job) + 1)

        def wait_emptied(eng, c, job):
            a, v = emptied(jobs_of(c), job)
            if job in EMPTIED_BY_DVE:
                eng.wait_ge(dve_emptied, base(c)[2] + v)
            else:
                eng.wait_ge(act_emptied, base(c)[1] + a)

        block = ctx.enter_context(nc.Block())

        @block.sync
        def _(sp):
            sp.dma_start(x_sb[:, 0], xv_dram[:, 0:TPC, :]).then_inc(x_first, 16)
            sp.dma_start(win[:, :], W_in[:, :]).then_inc(w_in, 16)
            sp.dma_start(rows[V_A:V_A + 32, :], A_log.rearrange("(g d) s -> g (d s)", d=GD)).then_inc(w_in, 16)
            sp.dma_start(rows[V_B1:V_B1 + 16, :], b1.rearrange("e (b p) -> (e b) p", p=P)).then_inc(w_in, 16)
            sp.dma_start(rows[V_BDT:V_BDT + 2, :], b_dt.rearrange("(b p) -> b p", p=P)).then_inc(w_in, 16)
            sp.dma_start(rows[V_CB:V_CB + 2, :], conv_b.rearrange("(b p) -> b p", p=P)).then_inc(w_in, 16)
            sp.dma_start(rows[V_DS:V_DS + 2, :], D_skip.rearrange("(b p) -> b p", p=P)).then_inc(w_in, 16)
            sp.dma_start(rows[V_NW:V_NW + 1, :], norm_w.rearrange("(b p) -> b p", p=P)).then_inc(w_in, 16)
            sp.dma_start(parts[:, 0, 0, 0:2, :].rearrange("p a b -> p (a b)"),
                         conv_w.rearrange("d a k -> a (d k)").to_broadcast([P, DIN * TAPS])).then_inc(w_in, 16)
            sp.dma_start(wx[:, :, :], W_x.rearrange("(b p) n -> p b n", p=P)).then_inc(w_in, 16)
            sp.dma_start(wdt[0:RANK, :], W_dt[:, :]).then_inc(w_in, 16)
            sp.dma_start(wout[:, :, :], W_out.rearrange("(b p) n -> p b n", p=P)).then_inc(w_in, 16)
            sp.dma_start(wg[:, :], Wg[:, :]).then_inc(w_in, 16)
            sp.dma_start(x_sb[:, 1:CHUNKS], xv_dram[:, TPC:CHUNKS * TPC, :].rearrange("p (c t) d -> p c t d", t=TPC)).then_inc(x_rest, 16)
            sp.dma_start(w1[:, :, :], W1.rearrange("e d h -> d e h")).then_inc(w_moe, 16)
            sp.dma_start(w2[:, :, :, :], W2.rearrange("e (b p) d -> p e b d", p=P)).then_inc(w_moe, 16)
            sp.wait_ge(consts, 2)
            for i in range(TPC):
                sp.dma_start(b2d[i * EXPERTS:(i + 1) * EXPERTS, i, :], b2[:, :]).then_inc(w_moe, 16)

            def restack(k):
                for b in range(DB):
                    if k > 0:
                        sp.wait_ge(dt_spread, UNITS * (k - 1) + (b + 1) * UNITS // DB)
                        sp.wait_ge(u_spread, UNITS * (k - 1) + (b + 1) * UNITS // DB)
                    for p in range(3):
                        sp.wait_ge(*((far_done, k + 1), (r1_done, DB * k + b + 1), (r2_done, DB * k + b + 1))[p])
                        for q in range(NQ):
                            sp.dma_start(stack[32 * p:32 * p + 32, b, q, :, :],
                                         parts[32 * q:32 * q + 32, b, :, p, :]).then_inc(stacked[b], 16)

            for k in range(CHUNKS):
                restack(k)
            for k in range(CHUNKS):
                sp.wait_ge(o_done, k + 1)
                sp.dma_start(ov_dram[:, k * TPC:(k + 1) * TPC, :],
                             xn[:, k]).then_inc(stored, 16)
            sp.wait_ge(stored, 16 * CHUNKS)

        @block.gpsimd
        def _(pool):
            pool.memset(ident[:, :], 0.0).then_inc(consts, 1)
            pool.memset(b2d[:, :, :], 0.0).then_inc(consts, 1)
            pool.memset(mhalf[:, :], -0.5).then_inc(consts, 1)
            pool.memset(own[:, :], 1.0).then_inc(consts, 1)
            pool.wait_ge(consts, 4)
            pool.affine_select(out=ident[:, :], in_=ident[:, :], compare_op=ALU.not_equal, fill=1.0,
                               base=0, pattern=[[-1, P]], channel_multiplier=1).then_inc(consts, 1)
            pool.affine_select(out=own[:, :], in_=own[:, :], compare_op=ALU.is_ge, fill=0.0,
                               base=0, pattern=[[-STATES, GD]], channel_multiplier=1).then_inc(consts, 1)
            pool.wait_ge(consts, 6)
            pool.affine_select(out=own[:, :], in_=own[:, :], compare_op=ALU.is_ge, fill=0.0,
                               base=STATES - 1, pattern=[[STATES, GD]], channel_multiplier=-1).then_inc(consts, 1)
            for e in range(EXPERTS):
                pool.memset(iota8[:, :, e:e + 1], float(e)).then_inc(consts, 1)

            def inverse_root(g, have, n, src, scale, mid, mid_sem, dst, dst_sem):
                t = slice(NORM[g].start, NORM[g].stop)
                pool.wait_ge(have, n)
                pool.tensor_scalar(mid[:, t], src[:, t], scale, EPS, ALU.mult, ALU.add).then_inc(mid_sem, 1)
                pool.wait_ge(mid_sem, g + 1)
                pool.tensor_tensor(dst[:, t], mid[:, t], mhalf[:, t], ALU.pow).then_inc(dst_sem, 1)

            def softplus_sum(k):
                pool.wait_ge(l_done, k + 1)
                pool.wait_ge(corr_done, k + 1)
                pool.tensor_tensor(lg1p[:, :, :], lg1p[:, :, :], corr[:, :, :], ALU.subtract).then_inc(lsum_done, 1)
                pool.wait_ge(lsum_done, k + 1)
                if k > 0:
                    for b in range(DB):
                        pool.wait_ge(stacked[b], 16 * 3 * NQ * k)
                pool.tensor_tensor(parts[:, :, 0, 0, :], lg1p[:, :, :], rl[:, :, :], ALU.add).then_inc(dt_done, 1)

            def times_C(c, n):
                c, n = c + n // UNITS, n % UNITS
                u = UNITS * c + n
                pool.wait_ge(scan_done, u + 1)
                if u >= 2 * PACK:
                    pool.wait_ge(reduced, u // PACK - 1)
                pool.tensor_tensor(hc[:, n % (2 * PACK), :], hs[:, u % 3, :], Ct[:, c % 2, :], ALU.mult)\
                    .then_inc(hc_done, 1)

            def finish(c):
                pool.wait_ge(g_done, c + 1)
                wait_emptied(pool, c, "o")
                pool.tensor_tensor(s_sb[:, c, :], s_sb[:, c, :], acc[:, c, :], ALU.mult).then_inc(sg_done, 1)
                pool.wait_ge(sg_done, c + 1)
                pool.tensor_tensor(s_sb[:, c, :], s_sb[:, c, :],
                                   x_sb[:, c].rearrange("p t d -> p (t d)"), ALU.add).then_inc(o_done, 1)

            for g in range(2):
                inverse_root(g, ln_mv, g + 1, mv[:, :, 1], 1.0, ve, ln_ve, rstd, ln_rstd)
                inverse_root(g, rms_sq, NORM[g].stop, ms, 1.0 / D, me, rms_me, rr, rms_r)
            softplus_sum(0)
            for n in range(HEAD):
                times_C(0, n)
            for c in range(CHUNKS):
                for n in range(HEAD, HEAD + UNITS if c < CHUNKS - 1 else UNITS):
                    times_C(c, n)
                    if c < CHUNKS - 1:
                        if n == 16:
                            softplus_sum(c + 1)
                    elif n in (17, 20, 23):
                        finish((n - 17) // 3)
            finish(CHUNKS - 1)

        @block.scalar
        def _(act):
            act.preload_act_table_set("natural_log_exp_and_others")
            act.wait_ge(vec_t, 1)
            act.activation(cols[:, :], px[0][:, 0:V_END], ACT.Copy).then_inc(vec_c, 1)
            act.wait_ge(vec_c, 1)
            act.activation(negA[:, :], cols[:, V_A:V_A + 32], ACT.Exp).then_inc(expA, 1)

            def squares(g):
                act.wait_ge(ln_xn, g + 1)
                for i in NORM[g]:
                    if i >= 2:
                        act.wait_ge(rms_sq, i - 1)
                    last = act.activation(sq[:, i % 2, :], xn[:, i // TPC, i % TPC, :], ACT.Square,
                                          accum_out=ms[:, i:i + 1]).then_inc(rms_sq, 1)

            def decay(c, n):
                c, n = c + n // UNITS, n % UNITS
                if c == CHUNKS:
                    return
                u = UNITS * c + n
                b, gl, q = n // (GL * NQ), n // NQ % GL, n % NQ
                g = (b * NQ + q) * GL + gl
                act.wait_ge(dt_spread, u + 1)
                act.activation(pd[n % 2][:, :], pd[n % 2][:, :], ACT.Exp, scale=negA[:, g:g + 1]).then_inc(decay_done, 1)

            def silu(k):
                act.preload_act_table_set("silu_and_others")
                wait_emptied(act, k - 1, "z1")
                if k >= 2:
                    act.wait_ge(yg_done, DB * (k - 1))
                act.activation(xc[:, k % 2], xv[:, :, :], ACT.Silu).then_inc(silu_done, 1)
                act.activation(sz[:, k % 2], zr[:, :, :], ACT.Silu).then_inc(silu_done, 1)
                act.preload_act_table_set("natural_log_exp_and_others")

            def log1p_exp(k):
                wait_emptied(act, k - 1, "v1")
                act.activation(ev[:, :, :], ev[:, :, :], ACT.Exp, scale=-1.0).then_inc(e_done, 1)
                act.wait_ge(e_done, k + 1)
                act.activation(lg1p[:, :, :], ev[:, :, :], ACT.Ln, bias=1.0).then_inc(l_done, 1)

            def empty(c, job):
                if job in EMPTIED_BY_DVE:
                    return
                k = c + 1
                src = bank_of(c, job)
                j = base(c)[0] + jobs_of(c).index(job)
                wait_filled(act, c, job)
                if job == "tn":
                    if c >= 0:
                        wait_emptied(act, c - 1, "gl")
                        act.wait_ge(xnT_copied, c + 1)
                    ins = act.activation(xnT_next[:, :], src[:, :], ACT.Copy)
                elif job == "tr":
                    ins = act.activation(xrT[:, :, PAD:PAD + SEQ], src[:, :].rearrange("p (b t) -> p b t", b=BPC),
                                         ACT.Copy, scale=cols[:, V_NW:V_NW + 1])
                elif job in ("z0", "z1"):
                    if k > 0:
                        act.wait_ge(dt_done, k)
                    ins = act.activation(zr[:, int(job[1]), :], src[:, :], ACT.Copy)
                elif job in ("xc0", "xc1"):
                    b = int(job[2])
                    if k > 0:
                        act.wait_ge(lsum_done, k)
                    ins = act.activation(xv[:, b, :], src[:, :], ACT.Identity, bias=cols[:, V_CB + b:V_CB + b + 1])
                elif job == "dt":
                    ins = act.activation(dtp[:, :], src[:, :], ACT.Copy)
                elif job == "B":
                    if k >= 2:
                        act.wait_ge(dbu_done, UNITS * (k - 1))
                    ins = act.activation(Bt[:, k % 2, :], src[:, :], ACT.Copy)
                elif job == "C":
                    if k >= 2:
                        act.wait_ge(hc_done, UNITS * (k - 1))
                    ins = act.activation(Ct[:, k % 2, :], src[:, :], ACT.Copy)
                elif job in ("v0", "v1"):
                    b = int(job[1])
                    if k > 0:
                        act.wait_ge(corr_done, k)
                        act.wait_ge(dt_done, k)
                    act.activation(rl[:, b, :], src[:, :], ACT.Relu, bias=cols[:, V_BDT + b:V_BDT + b + 1])
                    ins = act.activation(ev[:, b, :], src[:, :], ACT.Abs, bias=cols[:, V_BDT + b:V_BDT + b + 1])
                elif job == "gs":
                    ins = act.activation(sT[:, :], src[0:TPC * EXPERTS, 0:P], ACT.Copy)
                elif job == "gb":
                    ins = act.activation(acc[:, k, :], src[:, :], ACT.Copy)
                elif job[0] == "m":
                    e, b = int(job[1]), "ab".index(job[2])
                    if e >= 2:
                        act.wait_ge(filled, base(c)[0] + jobs_of(c).index(f"y{e - 2}") + 1)
                    elif c > 0:
                        act.wait_ge(filled, base(c - 1)[0] + jobs_of(c - 1).index(f"y{e + 6}") + 1)
                    ins = act.activation(hT[:, e % 2, b, :], src[:, :], ACT.Relu,
                                         bias=cols[:, V_B1 + HB * e + b:V_B1 + HB * e + b + 1])
                else:
                    ins = act.activation(nops[:, j:j + 1], src[:, 0:1], ACT.Copy)
                ins.then_inc(act_emptied, 1)

            def gate_e(k):
                wait_emptied(act, k - 1, "gl")
                act.activation(gex[:, :, :], glc[:, :, :], ACT.Exp).then_inc(gate_exp, 1)

            def copy_xnT(c):
                wait_emptied(act, c - 1, "tn")
                if c > 0:
                    wait_emptied(act, c - 1, "m7b")
                act.activation(xnT[:, :], xnT_next[:, :], ACT.Copy).then_inc(xnT_copied, 1)

            squares(0)
            for job in PRE_JOBS:
                if job == "xc1":
                    squares(1)
                if job == "dt":
                    silu(0)
                    gate_e(0)
                empty(-1, job)
                if job == "v1":
                    log1p_exp(0)
            copy_xnT(0)
            decay(0, 0)
            for n in range(HEAD):
                decay(0, n + 1)
            for c in range(CHUNKS):
                more = c < CHUNKS - 1
                if c > 0:
                    copy_xnT(c)
                for n in range(HEAD, HEAD + UNITS if more else UNITS + HEAD):
                    decay(c, n + 1) if more or n < UNITS else None
                    if more and n == 20:
                        gate_e(c + 1)
                    if more and n == 12:
                        silu(c + 1)
                    for job in SLOTS[n]:
                        if job in jobs_of(c):
                            empty(c, job)
                    if more and n == 15:
                        log1p_exp(c + 1)
                    if not more and n == 12:
                        act.preload_act_table_set("silu_and_others")
                        for k in range(CHUNKS - 1):
                            wait_emptied(act, k, "y7")
                            act.activation(acc[:, k, :], acc[:, k, :], ACT.Silu).then_inc(g_done, 1)
                        act.preload_act_table_set("natural_log_exp_and_others")
            act.preload_act_table_set("silu_and_others")
            wait_emptied(act, CHUNKS - 1, "y7")
            act.activation(acc[:, CHUNKS - 1, :], acc[:, CHUNKS - 1, :], ACT.Silu).then_inc(g_done, 1)

        @block.vector
        def _(dve):
            dve.memset(xrT[:, :, 0:PAD], 0.0).then_inc(setup, 1)
            dve.memset(wR[:, :, :], 0.0).then_inc(setup, 1)
            dve.memset(wdt[RANK:P, :], 0.0).then_inc(setup, 1)
            dve.memset(rsel[:, :, :], 0.0).then_inc(setup, 1)

            def stats(g):
                dve.wait_ge((x_first, x_rest)[g], 16)
                for i in NORM[g]:
                    last = dve.bn_stats(st[:, i, :], x_sb[:, i // TPC, i % TPC, :])
                last.then_inc(ln_st, 1)
                dve.wait_ge(ln_st, g + 1)
                for i in NORM[g]:
                    last = dve.bn_aggr(mv[:, i, :], st[:, i, :])
                last.then_inc(ln_mv, 1)

            def normalise(g):
                dve.wait_ge(ln_mv, g + 1)
                dve.wait_ge(ln_rstd, g + 1)
                for i in NORM[g]:
                    c, t = i // TPC, i % TPC
                    last = dve.tensor_scalar(xn[:, c, t, :], x_sb[:, c, t, :], mv[:, i, 0:1], rstd[:, i:i + 1],
                                             ALU.subtract, ALU.mult)
                last.then_inc(ln_xn, 1)

            def scale_rows(k):
                g = min(k, 1)
                dve.wait_ge(ln_xn, g + 1)
                dve.wait_ge(rms_r, g + 1)
                if k > 0:
                    wait_emptied(dve, k - 2, "tr")
                for i in range(TPC):
                    t = TPC * k + i
                    last = dve.tensor_scalar(xr[:, i, :], xn[:, k, i, :], rr[:, t:t + 1], None, ALU.mult)
                last.then_inc(rms_xr, 1)

            stats(0)
            normalise(0)
            dve.wait_ge(w_in, 16 * N_WIN)
            for t in range(TAPS):
                dve.tensor_tensor(wtap[:, t, :], win[:, 0:DIN], cwb[:, :, t], ALU.mult).then_inc(setup, 1)
            scale_rows(0)
            dve.wait_ge(setup, 8)
            for b in range(DB):
                for w, o in ((wB, RANK), (wC, RANK + STATES)):
                    dve.tensor_copy(w[:, b], wx[:, b, None, o:o + STATES].to_broadcast([P, GD, STATES])).then_inc(setup, 1)
                dve.tensor_copy(wR[:, b, 0:RANK], wx[:, b, 0:RANK]).then_inc(setup, 1)
            dve.wait_ge(consts, 7)
            for p in range(3):
                s = slice(32 * p, 32 * p + 32)
                dve.tensor_copy(sel[s, :, :, :].rearrange("p g d s -> p (g d) s"),
                                ident[s, s, None].to_broadcast([32, 32, STATES])).then_inc(setup, 1)
            for g in range(GL):
                dve.tensor_copy(rsel[:, g, g * GD:(g + 1) * GD], own[:, :]).then_inc(setup, 1)
            dve.wait_ge(expA, 1)
            dve.tensor_scalar(negA[:, :], negA[:, :], -1.0, None, ALU.mult).then_inc(setup, 1)

            def gate(k):
                n = [GATE_STEPS * k]

                def link(ins):
                    n[0] += 1
                    ins.then_inc(gate_step, 1)
                    dve.wait_ge(gate_step, n[0])

                src = bank_of(k - 1, "gl")[:, 0:TPC * EXPERTS].rearrange("p (t e) -> p t e", e=EXPERTS)
                wide = [P, TPC, EXPERTS]
                wait_filled(dve, k - 1, "gl")
                link(dve.tensor_reduce(gmx[:, :], src, AX.X, ALU.max))
                dve.tensor_tensor(glc[:, :, :], src, gmx[:, :, None].to_broadcast(wide), ALU.subtract).then_inc(dve_emptied, 1)
                yield
                dve.wait_ge(gate_exp, k + 1)
                link(dve.tensor_reduce(gsm[:, :], gex[:, :, :], AX.X, ALU.add))
                link(dve.reciprocal(gri[:, :], gsm[:, :]))
                link(dve.tensor_tensor(gp[:, :, :], gex[:, :, :], gri[:, :, None].to_broadcast(wide), ALU.mult))
                for i in range(TPC):
                    last = dve.max(gv8[:, i, :], gp[:, i, :])
                link(last)
                for i in range(TPC):
                    last = dve.max_index(gi8[:, i, :], gv8[:, i, :], gp[:, i, :])
                link(last)
                yield
                link(dve.tensor_copy(gif[:, :, :], gi8[:, :, 0:2]))
                link(dve.tensor_tensor(gs2[:, :], gv8[:, :, 0], gv8[:, :, 1], ALU.add))
                link(dve.reciprocal(grs[:, :], gs2[:, :]))
                link(dve.tensor_tensor(gvn[:, :, :], gv8[:, :, 0:2], grs[:, :, None].to_broadcast([P, TPC, 2]), ALU.mult))
                for j in range(2):
                    last = dve.tensor_tensor(goh[:, j], iota8[:, :, :], gif[:, :, j:j + 1].to_broadcast(wide), ALU.is_equal)
                link(last)
                for j in range(2):
                    last = dve.tensor_tensor(gw[:, j], goh[:, j], gvn[:, :, j:j + 1].to_broadcast(wide), ALU.mult)
                link(last)
                link(dve.tensor_tensor(score[:, k % 2], gw[:, 0], gw[:, 1], ALU.add))
                assert n[0] == GATE_STEPS * (k + 1), n[0]
                yield

            def correction(k):
                dve.wait_ge(e_done, k + 1)
                dve.tensor_scalar(corr[:, :, :], ev[:, :, :], 1.0, -1.0, ALU.add, ALU.add).then_inc(round_done, 1)
                dve.wait_ge(round_done, k + 1)
                dve.tensor_tensor(corr[:, :, :], corr[:, :, :], ev[:, :, :], ALU.subtract).then_inc(corr_done, 1)

            def upper(t):
                return t.bitcast(BF16).rearrange("p a b (t two) -> p a b t two", two=2)[:, :, :, :, 1]

            def times_dt(k):
                dve.wait_ge(dt_done, k + 1)
                dve.tensor_tensor(parts[:, :, 1, 0, :], parts[:, :, 0, 0, :], xc[:, k % 2], ALU.mult).then_inc(u_done, 1)
                dve.wait_ge(u_done, k + 1)
                dve.memset(parts[:, :, 0, 0, SEQ:CH:SEQ], FAR).then_inc(far_done, 1)
                dve.wait_ge(far_done, k + 1)

            def split(k, b, first):
                p = 0 if first else 1
                if not first:
                    dve.wait_ge(r1_done, DB * k + b + 1)
                src = parts[:, b, :, p, :]
                up = src.bitcast(BF16).rearrange("p a (t two) -> p a t two", two=2)[:, :, :, 1]
                ins = dve.tensor_tensor(parts[:, b, :, p + 1, :], src, up, ALU.subtract)
                if first:
                    ins.then_inc(r1_done, 1)
                else:
                    ins.then_inc(r2_done, 1)

            def times_B(c, n):
                c, n = c + n // UNITS, n % UNITS
                if c == CHUNKS:
                    return
                u = UNITS * c + n
                dve.wait_ge(u_spread, u + 1)
                if u >= 2:
                    dve.wait_ge(scan_done, u - 1)
                dve.tensor_tensor(dbu[:, n % 2, :], pu[n % 2][:, :], Bt[:, c % 2, :], ALU.mult).then_inc(dbu_done, 1)

            def scan(c, n):
                c, n = c + n // UNITS, n % UNITS
                u = UNITS * c + n
                dve.wait_ge(decay_done, u + 1)
                dve.wait_ge(dbu_done, u + 1)
                if u >= 3:
                    dve.wait_ge(hc_done, u - 2)
                dve.tensor_tensor_scan(hs[:, u % 3, :], pd[n % 2][:, :], dbu[:, n % 2, :], 0.0, ALU.mult, ALU.add)\
                    .then_inc(scan_done, 1)

            def gate_y(c, b):
                i = DB * c + b
                dve.wait_ge(reduced, UNITS // PACK * c + (b + 1) * UNITS // PACK // DB)
                if c > 0:
                    wait_emptied(dve, c - 1, "o")
                dve.scalar_tensor_tensor(yg[:, b, :], xc[:, c % 2, b, :], cols[:, V_DS + b:V_DS + b + 1], py[:, :],
                                         ALU.mult, ALU.add).then_inc(y_taken, 1)
                dve.wait_ge(y_taken, i + 1)
                dve.tensor_tensor(yg[:, b, :], yg[:, b, :], sz[:, c % 2, b, :], ALU.mult).then_inc(yg_done, 1)

            def empty(c, job):
                if job[0] == "y":
                    e = int(job[1])
                    src = bank_of(c, job)
                    wait_filled(dve, c, job)
                    wait_emptied(dve, *((c, f"y{e - 1}") if e > 0 else (c - 1, "gb")))
                    for i in range(TPC):
                        t = slice(i * D, (i + 1) * D)
                        last = dve.scalar_tensor_tensor(acc[:, c, t], src[:, t], score[:, c % 2, i, e:e + 1],
                                                        acc[:, c, t], ALU.mult, ALU.add)
                    last.then_inc(dve_emptied, 1)
                elif job == "o":
                    wait_filled(dve, c, job)
                    dve.tensor_tensor(s_sb[:, c, :], bank_of(c, job)[:, :], xn[:, c].rearrange("p t d -> p (t d)"),
                                      ALU.add).then_inc(dve_emptied, 1)

            stats(1)
            normalise(1)
            for _ in gate(0):
                pass
            correction(0)
            times_dt(0)
            for b in range(DB):
                split(0, b, True)
                split(0, b, False)
            times_B(0, 0)
            for n in range(HEAD):
                times_B(0, n + 1)
                scan(0, n)
            for c in range(CHUNKS):
                more = c < CHUNKS - 1
                gates = gate(c + 1) if more else None
                for n in range(HEAD, HEAD + UNITS):
                    if more or n < UNITS:
                        times_B(c, n + 1)
                        scan(c, n)
                    if n in SUM_Y:
                        gate_y(c, SUM_Y.index(n))
                    if more:
                        if n == 5:
                            scale_rows(c + 1)
                        if n in (19, 20, 21):
                            next(gates)
                        if n == 16:
                            correction(c + 1)
                        if n == 20:
                            times_dt(c + 1)
                        if n in (21, 23):
                            split(c + 1, (n - 21) // 2, True)
                        if n in (22, 24):
                            split(c + 1, (n - 22) // 2, False)
                    for job in SLOTS.get(n - 1, []):
                        if job in jobs_of(c) and job in EMPTIED_BY_DVE:
                            empty(c, job)
                for job in SLOTS[HEAD + UNITS - 1]:
                    empty(c, job)

        @block.tensor
        def _(pe):
            pe.wait_ge(w_in, 16 * N_WIN)
            pe.wait_ge(consts, 7)
            pe.transpose(px[0][:, 0:V_END], rows[:, :], ident[0:V_END, 0:V_END]).then_inc(vec_t, 1)

            def spread(c, n, kind):
                c, n = c + n // UNITS, n % UNITS
                if c == CHUNKS:
                    return
                u = UNITS * c + n
                b, gl, q = n // (GL * NQ), n // NQ % GL, n % NQ
                if n % (GL * NQ) == 0 and kind == 1:
                    pe.wait_ge(stacked[b], 16 * 3 * NQ * (c + 1))
                w = sel[:, gl].rearrange("p d s -> p (d s)")
                dst, used, done = ((pd, scan_done, dt_spread), (pu, dbu_done, u_spread))[kind]
                if u >= 2:
                    pe.wait_ge(used, u - 1)
                up = stack[0:96, b, q, kind, :].bitcast(BF16).rearrange("p (t two) -> p t two", two=2)[:, :, 1]
                pe.matmul(dst[n % 2][:, :], w, up, start=True, stop=True).then_inc(done, 1)

            def reduce_pack(c, m):
                b, gl = m // GL, m % GL
                pe.wait_ge(hc_done, UNITS * c + PACK * (m + 1))
                if gl == 0 and DB * c + b > 0:
                    pe.wait_ge(y_taken, DB * c + b)
                for q in range(NQ):
                    last = pe.matmul(py[32 * q:32 * q + 32, :], rsel[:, gl, :], hc[:, (PACK * m + q) % (2 * PACK), :],
                                     start=gl == 0, stop=gl == GL - 1)
                last.then_inc(reduced, 1)

            def fill(c, job):
                halves = {"<": 0}.get(job[-1])
                second = c >= 0 and job + "<" in STARTED
                job = job.rstrip("<")
                jobs, k = jobs_of(c), c + 1
                j = jobs.index(job)
                dst = px[j % AUX]
                if j >= AUX:
                    wait_emptied(pe, c, jobs[j - AUX])
                elif c >= 0:
                    pe.wait_ge(act_emptied, base(c)[1])
                    pe.wait_ge(dve_emptied, base(c)[2])
                elif j == 0:
                    pe.wait_ge(vec_c, 1)
                if job == "tn":
                    pe.wait_ge(ln_xn, min(k, 1) + 1)
                    for i in range(TPC):
                        last = pe.transpose(dst[:, i * P:(i + 1) * P], xn[:, k, i, :], ident[:, :])
                elif job == "tr":
                    pe.wait_ge(rms_xr, k + 1)
                    for i in range(TPC):
                        last = pe.transpose(dst[:, i * P:(i + 1) * P], xr[:, i, :], ident[:, :])
                elif job in ("z0", "z1"):
                    wait_emptied(pe, c, "tr")
                    o = DIN + int(job[1]) * P
                    last = pe.matmul(dst[:, :], win[:, o:o + P], xrT[:, :, PAD:PAD + SEQ], start=True, stop=True)
                elif job in ("xc0", "xc1"):
                    wait_emptied(pe, c, "tr")
                    if c < 0:
                        pe.wait_ge(setup, 8)
                    b = int(job[2])
                    for t in (range(2) if halves == 0 else range(2, TAPS) if second else range(TAPS)):
                        last = pe.matmul(dst[:, :], wtap[:, t, b * P:(b + 1) * P], xrT[:, :, t:t + SEQ],
                                         start=t == 0, stop=t == TAPS - 1)
                elif job in ("dt", "B", "C"):
                    pe.wait_ge(silu_done, 2 * k + 1)
                    if c < 0:
                        pe.wait_ge(setup, 14)
                    for b in range(DB):
                        w = {"dt": wR[:, b, :], "B": wB[:, b].rearrange("p d s -> p (d s)"),
                             "C": wC[:, b].rearrange("p d s -> p (d s)")}[job]
                        last = pe.matmul(dst[:, :], w, xc[:, k % 2, b, :], start=b == 0, stop=b == DB - 1)
                elif job in ("v0", "v1"):
                    wait_emptied(pe, c, "dt")
                    b = int(job[1])
                    last = pe.matmul(dst[:, :], wdt[:, b * P:(b + 1) * P], dtp[:, :], start=True, stop=True)
                elif job == "gl":
                    wait_emptied(pe, c, "tn")
                    for i in range(TPC):
                        last = pe.matmul(dst[:, i * EXPERTS:(i + 1) * EXPERTS], xnT_next[:, i * P:(i + 1) * P], wg[:, :],
                                         start=True, stop=True)
                elif job == "gs":
                    pe.wait_ge(gate_step, GATE_STEPS * (k + 1))
                    last = pe.transpose(dst[0:TPC * EXPERTS, 0:P], score[:, k % 2].rearrange("p t e -> p (t e)"), ident[:, :])
                elif job == "gb":
                    wait_emptied(pe, c, "gs")
                    if c < 0:
                        pe.wait_ge(w_moe, 16 * 6)
                    last = pe.matmul(dst[:, :], sT[:, :], b2d[:, :, :].rearrange("e t d -> e (t d)"), start=True, stop=True)
                elif job[0] == "m":
                    e, b = int(job[1]), "ab".index(job[2])
                    pe.wait_ge(xnT_copied, c + 1)
                    last = pe.matmul(dst[:, :], w1[:, e, b * P:(b + 1) * P], xnT[:, :], start=True, stop=True)
                elif job[0] == "y":
                    e = int(job[1])
                    wait_emptied(pe, c, f"m{e}b")
                    for i in range(TPC):
                        for b in range(HB):
                            last = pe.matmul(dst[:, i * D:(i + 1) * D], hT[:, e % 2, b, i * P:(i + 1) * P], w2[:, e, b, :],
                                             start=b == 0, stop=b == HB - 1)
                elif job == "o":
                    pe.wait_ge(yg_done, DB * (c + 1))
                    for i in range(TPC):
                        for b in range(DB):
                            last = pe.matmul(dst[:, i * D:(i + 1) * D], yg[:, b, i * P:(i + 1) * P], wout[:, b, :],
                                             start=b == 0, stop=b == DB - 1)
                else:
                    last = pe.matmul(dst[:, 0:EXPERTS], ident[:, :], wg[:, :], start=True, stop=True)
                if halves is None:
                    last.then_inc(filled, 1)

            for job in PRE_JOBS:
                fill(-1, job)
            pe.wait_ge(setup, 22)
            for n, kind in ((0, 1), (1, 1), (0, 0)):
                spread(0, n, kind)
            for n in range(HEAD):
                spread(0, n + 1, 0)
                spread(0, n + 2, 1)
            for c in range(CHUNKS):
                more = c < CHUNKS - 1
                for n in range(HEAD, HEAD + UNITS):
                    if more or n < UNITS:
                        spread(c, n + 1, 0)
                        spread(c, n + 2, 1)
                    if (n - LAG) % PACK == PACK - 1:
                        reduce_pack(c, (n - LAG) // PACK)
                    for job in SLOTS[n]:
                        if job.rstrip("<") in jobs_of(c):
                            fill(c, job)


_INS = ["L0_attn_x", "L0_attn_norm_w", "L0_attn_W_in", "L0_attn_conv_w", "L0_attn_conv_b", "L0_attn_W_x",
        "L0_attn_W_dt", "L0_attn_b_dt", "L0_attn_A_log", "L0_attn_D_skip", "L0_attn_W_out",
        "L0_ffn_Wg", "L0_ffn_W1", "L0_ffn_b1", "L0_ffn_W2", "L0_ffn_b2"]


def kernel(**inputs):
    import numpy as np
    import concourse.bacc as bacc
    from concourse.bass_utils import run_bass_kernel_spmd

    nc = bacc.Bacc("TRN2", target_bir_lowering=False, num_devices=1)
    arrays, args = {}, []
    for name in _INS:
        a = np.ascontiguousarray(inputs[name])
        arrays[f"in_{name}"] = a
        args.append(nc.dram_tensor(f"in_{name}", a.shape, mybir.dt.from_np(a.dtype), kind="ExternalInput").ap())
    args.append(nc.dram_tensor("out_0", (BATCH, SEQ, D), F32, kind="ExternalOutput").ap())
    mamba_moe(nc, *args)
    r = run_bass_kernel_spmd(nc, [arrays], core_ids=[0])
    return r.results[0]["out_0"]
```

```python
from contextlib import ExitStack

import concourse.bass as bass
from concourse import mybir

ALU = mybir.AluOpType
ACT = mybir.ActivationFunctionType
AX = mybir.AxisListType
F32 = mybir.dt.float32
BF16 = mybir.dt.bfloat16
U32 = mybir.dt.uint32

P = 128
BATCH, SEQ, D = 8, 256, 128
DIN, STATES, RANK, TAPS = 256, 16, 64, 4
EXPERTS, HID = 8, 256
EPS = 1e-5
TOK = BATCH * SEQ
CH = 512
BPC = CH // SEQ
TPC = CH // P
CHUNKS = TOK // CH
TILES = TOK // P
NORM = [range(0, TPC), range(TPC, TILES)]
DB = DIN // P
GD = P // STATES
GL = 32 // GD
NQ = P // 32
UNITS = DB * GL * NQ
PACK = NQ
HB = HID // P
PAD = TAPS - 1
FAR = 1.0e28

V_A, V_B1, V_BDT, V_CB, V_DS, V_NW, V_END = 0, 32, 48, 50, 52, 54, 55

PRE_JOBS = ["tr", "xc0", "xc1", "dt", "v0", "tn", "B", "C", "v1", "m0a"]
EARLY = {0: ["m1a", "gl", "z0"], 2: ["m0b", "z1"], 3: ["m1b"], 5: ["gs"], 6: ["gb"]}
FIRST = {
    4: ["y0"], 5: ["tr"], 6: ["z1", "y1", "xc0<"], 8: ["xc0"], 9: ["m3a"], 10: ["xc1<"], 12: ["z0", "xc1"],
    13: ["m2b", "m2a", "dt", "tn"], 15: ["v0", "v1"], 17: ["gl", "m3b"], 18: ["y2"], 19: ["y3"],
    20: ["m4a"], 22: ["m5a"], 23: ["m5b", "m4b"], 24: ["y4"], 26: ["m6a", "y5", "m7a"], 28: ["m6b", "m7b"],
    29: ["gs"], 31: ["gb"], 32: ["y6"], 35: ["y7"], 36: ["o"],
}
MIDDLE = {
    5: ["tr", "m0b"], 6: ["xc0<"], 7: ["z0", "xc0"], 10: ["xc1"], 11: ["z1"], 13: ["dt"], 15: ["v0", "v1"],
    16: ["m1a", "m0a"], 17: ["m1b", "tn"], 18: ["y0", "gl"], 19: ["m2a"], 20: ["m2b", "y1"],
    21: ["m3a", "gs"], 22: ["m3b", "gb", "y2", "m4a"], 23: ["y3"], 24: ["m4b"], 26: ["m5b"],
    27: ["y4", "m5a"], 28: ["m6b"], 30: ["m6a"], 31: ["m7a"], 32: ["y5"], 33: ["y6", "m7b"], 35: ["o"],
    36: ["y7"],
}
LAST = {
    7: ["m0b", "m1a"], 8: ["m0a"], 11: ["m1b"], 15: ["y0", "m2a"], 16: ["y1"], 18: ["m2b"],
    20: ["m3b", "y2"], 22: ["m4b"], 23: ["m3a", "m4a"], 24: ["y3"], 26: ["m5b"], 27: ["y4"], 28: ["m5a"],
    30: ["y5", "m7b", "m6a"], 31: ["m7a"], 32: ["m6b"], 33: ["y6"], 34: ["y7"], 35: ["o"],
}
STEPS = [{
    "silu": [13], "log1p": [15, 15], "correct": [16, 16, 16, 16], "sum_dt": [15, 15], "times_dt": [18, 21],
    "split_1": [19, 19, 25, 25], "split_2": [22, 22, 26, 26], "scale_rows": [4], "normalise": [14],
    "gate": [19, 20, 20, 20, 21, 21], "gate_e": [19], "sum_y": [18, 34], "gate_z": [18, 34],
}, {
    "silu": [12], "log1p": [15, 15], "correct": [16, 16, 17, 19], "sum_dt": [16, 20], "times_dt": [18, 21],
    "split_1": [21, 21, 23, 24], "split_2": [22, 24, 25, 27], "scale_rows": [4], "normalise": [11],
    "gate": [19, 20, 20, 20, 20, 20], "gate_e": [20], "sum_y": [18, 33], "finish": [20], "gate_z": [20, 34],
}]
START = {
    "gate": [1, 1, 1, 3, 3, 3], "gate_e": [0], "correct": [0, 0], "sum_dt": [0], "times_dt": [6],
    "split_1": [6, 6], "split_2": [12, 13],
}
END = {"sum_y": [20, 31], "gate_z": [28, 35]}
LEAD = 2
LAG = 2
DVE_EXPERTS = [20, 30, 31]
AUX = 3
OWN = {"o"} | {f"y{e}" for e in range(EXPERTS)} | {f"m{e}{b}" for e in range(EXPERTS) for b in "ab"}
SLOTS = {n: [(j, 0) for j in EARLY[n]] for n in EARLY}
for c in range(CHUNKS):
    for n, jobs in (FIRST if c == 0 else MIDDLE if c < CHUNKS - 1 else LAST).items():
        SLOTS.setdefault(UNITS * c + n, []).extend((j, c if j in OWN else c + 1) for j in jobs)
SLOTS = {n: SLOTS[n] for n in sorted(SLOTS)}
JOBS = [(j, 0) for j in PRE_JOBS] + [(j, k) for n in SLOTS for j, k in SLOTS[n] if j[-1] != "<"]
STARTED = {(j[:-1], k) for n in SLOTS for j, k in SLOTS[n] if j[-1] == "<"}


def by_dve(job, k):
    return job in ("gl", "o") or (job, k) == ("xc0", 0) or job[0] == "y" and EXPERTS * k + int(job[1]) in DVE_EXPERTS


def place(u):
    n = u % UNITS
    return n // (GL * NQ), n // NQ % GL, n % NQ


END_SLOT = max(max(SLOTS), CHUNKS * UNITS + LAG)
GATE_STEPS = 13


def steps_at(n, name):
    found = [(0, i) for i, m in enumerate(START.get(name, [])) if m == n]
    for c in range(CHUNKS):
        table = END if c == CHUNKS - 1 else STEPS[min(c, 1)]
        found += [(c + 1, i) for i, m in enumerate(table.get(name, [])) if UNITS * c + m == n]
    return found


def mamba_moe(nc, x, norm_w, W_in, conv_w, conv_b, W_x, W_dt, b_dt, A_log, D_skip, W_out,
              Wg, W1, b1, W2, b2, out):
    with ExitStack() as ctx:
        def sb(name, shape, dt=F32):
            return ctx.enter_context(nc.sbuf_tensor(name, shape, dt))

        def sem(name):
            return ctx.enter_context(nc.semaphore(name))

        x_sb = sb("x_sb", [P, CHUNKS, TPC, D])
        xn = sb("xn", [P, CHUNKS, TPC, D])
        acc = sb("acc", [P, 3, CH])
        s_sb = xn[:, :, :, :].rearrange("p c t d -> p c (t d)")
        xnT = sb("xnT", [P, 2, CH])
        xrT = sb("xrT", [P, BPC, PAD + SEQ])
        zr = sb("zr", [P, DB, CH])
        xv = sb("xv", [P, DB, CH])
        sz = sb("sz", [P, 2, DB, CH])
        xc = sb("xc", [P, 2, DB, CH])
        Bt = sb("Bt", [P, 2, CH])
        Ct = sb("Ct", [P, 2, CH])
        dtp = sb("dtp", [P, CH])
        ev = sb("ev", [P, DB, CH])
        rl = sb("rl", [P, DB, CH])
        xr = rl[:, 0, :].rearrange("p (t d) -> p t d", d=D)
        lg1p, corr = zr, xv
        parts = sb("parts", [P, DB, 2, 3, CH])
        stack = sb("stack", [P, DB, NQ, 2, CH])
        win = sb("win", [P, 2 * DIN])
        wtap = sb("wtap", [P, TAPS, DIN])
        cwb = parts[:, 0, 0, 0:2, :].rearrange("p a b -> p (a b)").rearrange("p (d k) -> p d k", k=TAPS)
        cw = sb("cw", [P, TAPS])
        wx = sb("wx", [P, DB, RANK + 2 * STATES])
        wB = sb("wB", [P, DB, GD, STATES])
        wC = sb("wC", [P, DB, GD, STATES])
        wdt = sb("wdt", [P, DIN])
        wout = sb("wout", [P, DB, D])
        wg = sb("wg", [P, EXPERTS])
        w1 = sb("w1", [P, EXPERTS, HID])
        w2 = sb("w2", [P, EXPERTS, HB, D])
        b2d = sb("b2d", [TPC * EXPERTS, TPC, D])
        rows = sb("rows", [V_END, P])
        cols = sb("cols", [P, V_END])
        negA = sb("negA", [P, 32])
        ident = sb("ident", [P, P])
        own = sb("own", [P, GD])
        sel = sb("sel", [96, GL, GD, STATES], BF16)
        sel_first = sb("sel_first", [P, NQ, GD, STATES], BF16)
        rsel = sb("rsel", [P, GL, 32])
        iota8 = sb("iota8", [P, TPC, EXPERTS])
        mhalf = sb("mhalf", [P, TILES])
        st = sb("st", [P, TILES, 6])
        mv = sb("mv", [P, TILES, 2])
        ve = sb("ve", [P, TILES])
        rstd = sb("rstd", [P, TILES])
        me = sb("me", [P, TILES])
        rr = sb("rr", [P, TILES])
        gmx = sb("gmx", [P, TPC])
        glc = sb("glc", [P, TPC, EXPERTS])
        gex = sb("gex", [P, TPC, EXPERTS])
        gsm = sb("gsm", [P, TPC])
        gri = sb("gri", [P, TPC])
        gp = sb("gp", [P, TPC, EXPERTS])
        gv8 = sb("gv8", [P, TPC, 8])
        gi8 = sb("gi8", [P, TPC, 8], U32)
        gif = sb("gif", [P, TPC, 2])
        gs2 = sb("gs2", [P, TPC])
        grs = sb("grs", [P, TPC])
        gvn = sb("gvn", [P, TPC, 2])
        goh = sb("goh", [P, 2, TPC, EXPERTS])
        gw = sb("gw", [P, 2, TPC, EXPERTS])
        score = sb("score", [P, 2, TPC, EXPERTS])
        sT = sb("sT", [TPC * EXPERTS, P])
        dec = sb("dec", [P, 3, CH])
        dbu = sb("dbu", [P, 2, CH])
        hs = sb("hs", [P, 3, CH])
        hc = sb("hc", [P, 2 * PACK, CH])
        hT = sb("hT", [P, 2, HB, CH])
        ysc = sb("ysc", [P, CH])
        yg = sb("yg", [P, DB, CH])

        def bank(name):
            return ctx.enter_context(nc.psum_tensor(name, [P, CH], F32))

        pd = [bank(f"pd{i}") for i in range(2)]
        pu = [bank(f"pu{i}") for i in range(2)]
        py = bank("py")
        px = [bank(f"px{i}") for i in range(AUX)]

        x_first, x_rest = sem("x_first"), sem("x_rest")
        w_rows, w_tap, w_proj, w_moe = sem("w_rows"), sem("w_tap"), sem("w_proj"), sem("w_moe")
        consts = sem("consts")
        setup = sem("setup")
        vec_t, vec_c, expA, negated = sem("vec_t"), sem("vec_c"), sem("expA"), sem("negated")
        ln_mv, ln_ve, ln_rstd, ln_xn = sem("ln_mv"), sem("ln_ve"), sem("ln_rstd"), sem("ln_xn")
        ln_st = sem("ln_st")
        rms_me, rms_r, rms_xr = sem("rms_me"), sem("rms_r"), sem("rms_xr")
        silu_done, sz_done = sem("silu_done"), sem("sz_done")
        abs_done = sem("abs_done")
        conv_step, silu_first = sem("conv_step"), sem("silu_first")
        last_sg_done, last_done = sem("last_sg_done"), sem("last_done")
        acc_added = sem("acc_added")
        BC_there = sem("BC_there")
        e_done, l_done = sem("e_done"), sem("l_done")
        round_done, corr_done = sem("round_done"), sem("corr_done")
        lsum_done, dt_done = sem("lsum_done"), sem("dt_done")
        u_done, far_done, r1_done, r2_done = sem("u_done"), sem("far_done"), sem("r1_done"), sem("r2_done")
        stacked = [sem("stacked0"), sem("stacked1")]
        gate_exp, gate_step = sem("gate_exp"), sem("gate_step")
        filled = sem("filled")
        act_emptied, dve_emptied = sem("act_emptied"), sem("dve_emptied")
        dt_spread, u_spread = sem("dt_spread"), sem("u_spread")
        decay_done, dbu_done, scan_done, hc_done = sem("decay_done"), sem("dbu_done"), sem("scan_done"), sem("hc_done")
        reduced = sem("reduced")
        y_taken, yg_done = sem("y_taken"), sem("yg_done")
        g_done, sg_done, o_done, stored = sem("g_done"), sem("sg_done"), sem("o_done"), sem("stored")

        NBC = 2 * GD
        N_SETUP = 4 + TAPS + 2 * DB + NQ + 3 + GL
        N_ROWS, N_TAP, N_PROJ, N_MOE = 6, 3, 3, 3 + TPC
        xv_dram = x.rearrange("b (h p) d -> p (b h) d", p=P)
        ov_dram = out.rearrange("b (h p) d -> p (b h) d", p=P)

        order_a = [job for job in JOBS if not by_dve(*job)]
        order_v = [job for job in JOBS if by_dve(*job)]

        def bank_of(job, k):
            return px[JOBS.index((job, k)) % AUX]

        def wait_filled(eng, job, k):
            eng.wait_ge(filled, JOBS.index((job, k)) + 1)

        def wait_emptied(eng, job, k):
            if by_dve(job, k):
                eng.wait_ge(dve_emptied, order_v.index((job, k)) + 1)
            else:
                eng.wait_ge(act_emptied, order_a.index((job, k)) + 1)

        def wait_silu(eng, kind, k, b):
            if kind == "z":
                eng.wait_ge(sz_done, DB * k + b + 1)
            elif k == 0:
                eng.wait_ge(silu_first, 1) if b == 0 else wait_emptied(eng, "xc1", 0)
            else:
                eng.wait_ge(silu_done, DB * (k - 1) + b + 1)

        def wait_all_emptied(eng, jobs, k):
            wait_emptied(eng, max(jobs, key=lambda job: JOBS.index((job, k))), k)

        pool_experts = [(k, e) for k in range(CHUNKS) for e in range(EXPERTS) if not by_dve(f"y{e}", k)]

        def wait_added(eng, k, e):
            if e < 0:
                wait_emptied(eng, "gb", k)
            elif by_dve(f"y{e}", k):
                wait_emptied(eng, f"y{e}", k)
            else:
                eng.wait_ge(acc_added, pool_experts.index((k, e)) + 1)

        block = ctx.enter_context(nc.Block())

        @block.sync
        def _(sp):
            sp.dma_start(x_sb[:, 0], xv_dram[:, 0:TPC, :]).then_inc(x_first, 16)
            sp.dma_start(rows[V_NW:V_NW + 1, :], norm_w.rearrange("(b p) -> b p", p=P)).then_inc(w_rows, 16)
            sp.dma_start(rows[V_CB:V_CB + 2, :], conv_b.rearrange("(b p) -> b p", p=P)).then_inc(w_rows, 16)
            sp.dma_start(rows[V_A:V_A + 32, :], A_log.rearrange("(g d) s -> g (d s)", d=GD)).then_inc(w_rows, 16)
            sp.dma_start(rows[V_B1:V_B1 + 16, :], b1.rearrange("e (b p) -> (e b) p", p=P)).then_inc(w_rows, 16)
            sp.dma_start(win[:, :], W_in[:, :]).then_inc(w_tap, 16)
            sp.dma_start(wx[:, :, :], W_x.rearrange("(b p) n -> p b n", p=P)).then_inc(w_proj, 16)
            sp.dma_start(wdt[0:RANK, :], W_dt[:, :]).then_inc(w_proj, 16)
            sp.dma_start(wg[:, :], Wg[:, :]).then_inc(w_proj, 16)
            sp.dma_start(x_sb[:, 1:CHUNKS], xv_dram[:, TPC:TILES, :].rearrange("p (c t) d -> p c t d", t=TPC))\
                .then_inc(x_rest, 16)
            sp.dma_start(w1[:, :, :], W1.rearrange("e d h -> d e h")).then_inc(w_moe, 16)
            sp.dma_start(w2[:, :, :, :], W2.rearrange("e (b p) d -> p e b d", p=P)).then_inc(w_moe, 16)
            sp.dma_start(wout[:, :, :], W_out.rearrange("(b p) n -> p b n", p=P)).then_inc(w_moe, 16)
            sp.wait_ge(consts, 2)
            for i in range(TPC):
                sp.dma_start(b2d[i * EXPERTS:(i + 1) * EXPERTS, i, :], b2[:, :]).then_inc(w_moe, 16)

            def restack(k):
                for b in range(DB):
                    if k > 0:
                        sp.wait_ge(dt_spread, UNITS * (k - 1) + (b + 1) * UNITS // DB)
                        sp.wait_ge(u_spread, UNITS * (k - 1) + (b + 1) * UNITS // DB)
                    for p in range(3):
                        if p == 0:
                            sp.wait_ge(far_done, DB * k + b + 1)
                        else:
                            sp.wait_ge((r1_done, r2_done)[p - 1], 2 * (DB * k + b + 1))
                        for q in range(NQ):
                            sp.dma_start(stack[32 * p:32 * p + 32, b, q, :, :],
                                         parts[32 * q:32 * q + 32, b, :, p, :]).then_inc(stacked[b], 16)

            def repeat_BC(k):
                wait_emptied(sp, "dt", k)
                if k > 1:
                    sp.wait_ge(dbu_done, UNITS * (k - 1))
                    sp.wait_ge(hc_done, UNITS * (k - 1))
                for t, o in ((Bt, RANK), (Ct, RANK + STATES)):
                    for d in range(GD):
                        sp.dma_start(t[STATES * d:STATES * (d + 1), k % 2, :], dtp[o:o + STATES, :])\
                            .then_inc(BC_there, 16)

            for k in range(CHUNKS):
                if k > 0:
                    repeat_BC(k)
                restack(k)
            for k in range(CHUNKS):
                sp.wait_ge(*((o_done, k + 1) if k < CHUNKS - 1 else (last_done, 1)))
                sp.dma_start(ov_dram[:, k * TPC:(k + 1) * TPC, :], xn[:, k]).then_inc(stored, 16)
            sp.wait_ge(stored, 16 * CHUNKS)

        def times_C(eng, u):
            c = u // UNITS
            eng.wait_ge(scan_done, u + 1)
            if u >= 2 * PACK:
                eng.wait_ge(reduced, u // PACK - 1)
            if u % UNITS == 0:
                wait_emptied(eng, "C", 0) if c == 0 else eng.wait_ge(BC_there, 16 * NBC * c)
            eng.tensor_tensor(hc[:, u % (2 * PACK), :], hs[:, u % 3, :], Ct[:, c % 2, :], ALU.mult)\
                .then_inc(hc_done, 1)

        def softplus_sum(eng, k, b):
            eng.wait_ge(l_done, DB * k + b + 1)
            eng.wait_ge(corr_done, DB * k + b + 1)
            eng.tensor_tensor(lg1p[:, b, :], lg1p[:, b, :], corr[:, b, :], ALU.subtract).then_inc(lsum_done, 1)
            eng.wait_ge(lsum_done, DB * k + b + 1)
            if k > 0:
                eng.wait_ge(stacked[b], 16 * 3 * NQ * k)
            wait_emptied(eng, f"v{b}", k)
            eng.tensor_tensor(parts[:, b, 0, 0, :], lg1p[:, b, :], rl[:, b, :], ALU.add).then_inc(dt_done, 1)

        @block.gpsimd
        def _(pool):
            pool.memset(ident[:, :], 0.0).then_inc(consts, 1)
            pool.memset(b2d[:, :, :], 0.0).then_inc(consts, 1)
            pool.memset(mhalf[:, :], -0.5).then_inc(consts, 1)
            pool.memset(own[:, :], 1.0).then_inc(consts, 1)
            pool.wait_ge(consts, 4)
            pool.affine_select(out=ident[:, :], in_=ident[:, :], compare_op=ALU.not_equal, fill=1.0,
                               base=0, pattern=[[-1, P]], channel_multiplier=1).then_inc(consts, 1)
            pool.affine_select(out=own[:, :], in_=own[:, :], compare_op=ALU.is_ge, fill=0.0,
                               base=0, pattern=[[-STATES, GD]], channel_multiplier=1).then_inc(consts, 1)
            pool.wait_ge(consts, 6)
            pool.affine_select(out=own[:, :], in_=own[:, :], compare_op=ALU.is_ge, fill=0.0,
                               base=STATES - 1, pattern=[[STATES, GD]], channel_multiplier=-1).then_inc(consts, 1)
            for e in range(EXPERTS):
                pool.memset(iota8[:, :, e:e + 1], float(e)).then_inc(consts, 1)

            def inverse_roots(g):
                t = slice(NORM[g].start, NORM[g].stop)
                pool.wait_ge(ln_mv, g + 1)
                pool.tensor_scalar(me[:, t], mv[:, t, 1], 1.0 + EPS, EPS * EPS, ALU.mult, ALU.add).then_inc(rms_me, 1)
                pool.tensor_scalar(ve[:, t], mv[:, t, 1], 1.0, EPS, ALU.mult, ALU.add).then_inc(ln_ve, 1)
                pool.wait_ge(rms_me, g + 1)
                pool.tensor_tensor(rr[:, t], me[:, t], mhalf[:, t], ALU.pow).then_inc(rms_r, 1)
                pool.wait_ge(ln_ve, g + 1)
                pool.tensor_tensor(rstd[:, t], ve[:, t], mhalf[:, t], ALU.pow).then_inc(ln_rstd, 1)

            def finish(c):
                pool.wait_ge(g_done, c + 1)
                wait_emptied(pool, "o", c)
                pool.tensor_tensor(s_sb[:, c, :], s_sb[:, c, :], acc[:, c % 3, :], ALU.mult).then_inc(sg_done, 1)
                pool.wait_ge(sg_done, c + 1)
                pool.tensor_tensor(s_sb[:, c, :], s_sb[:, c, :],
                                   x_sb[:, c].rearrange("p t d -> p (t d)"), ALU.add).then_inc(o_done, 1)

            def add_expert(k, e):
                wait_added(pool, k, e - 1)
                wait_emptied(pool, f"y{e}", k)
                pool.tensor_tensor(acc[:, k % 3, :], acc[:, k % 3, :], ysc[:, :], ALU.add).then_inc(acc_added, 1)

            inverse_roots(0)
            inverse_roots(1)
            for n in range(END_SLOT + 2):
                for job, k in SLOTS.get(n - 1, []):
                    if job[0] == "y" and job[-1] != "<" and not by_dve(job, k):
                        add_expert(k, int(job[1]))
                if n < CHUNKS * UNITS - 1:
                    times_C(pool, n)
                for k, b in steps_at(n, "sum_dt"):
                    softplus_sum(pool, k, b + (k == 0))
                for k, _ in steps_at(n, "finish"):
                    finish(k - 2)
            finish(CHUNKS - 2)

        @block.scalar
        def _(act):
            act.dma_start(parts[:, 0, 0, 0:2, :].rearrange("p a b -> p (a b)"),
                          conv_w.rearrange("d a k -> a (d k)").to_broadcast([P, DIN * TAPS])).then_inc(w_tap, 16)
            act.dma_start(cw[:, :], conv_w.rearrange("(b p) a k -> p b (a k)", p=P)[:, 0]).then_inc(w_tap, 16)
            act.dma_start(rows[V_BDT:V_BDT + 2, :], b_dt.rearrange("(b p) -> b p", p=P)).then_inc(w_rows, 16)
            act.dma_start(rows[V_DS:V_DS + 2, :], D_skip.rearrange("(b p) -> b p", p=P)).then_inc(w_rows, 16)
            act.preload_act_table_set("silu_and_others")
            act.wait_ge(vec_t, 1)
            act.activation(cols[:, :], pd[0][:, 0:V_END], ACT.Copy).then_inc(vec_c, 1)
            act.wait_ge(vec_c, 1)

            def decay(u):
                b, gl, q = place(u)
                g = (b * NQ + q) * GL + gl
                act.wait_ge(dt_spread, u + 1)
                if u >= 3:
                    act.wait_ge(scan_done, u - 2)
                act.activation(dec[:, u % 3, :], pd[u % 2][:, :], ACT.Exp, scale=negA[:, g:g + 1])\
                    .then_inc(decay_done, 1)

            def silu_of_experts(k):
                wait_added(act, k, EXPERTS - 1)
                act.activation(acc[:, k % 3, :], acc[:, k % 3, :], ACT.Silu).then_inc(g_done, 1)

            def silu(k):
                act.preload_act_table_set("silu_and_others")
                if k == 1:
                    wait_all_emptied(act, ("z0", "z1"), 0)
                    act.activation(sz[:, 0], sz[:, 0], ACT.Silu).then_inc(sz_done, 2)
                wait_all_emptied(act, ("z0", "z1", "xc0", "xc1"), k)
                if k >= 2:
                    act.wait_ge(yg_done, DB * (k - 1))
                act.activation(xc[:, k % 2], xv[:, :, :], ACT.Silu).then_inc(silu_done, 2)
                act.activation(sz[:, k % 2], zr[:, :, :], ACT.Silu).then_inc(sz_done, 2)
                if k >= 2:
                    silu_of_experts(k - 2)
                act.preload_act_table_set("natural_log_exp_and_others")

            def log1p_exp(k, b):
                act.wait_ge(abs_done, DB * k + b + 1)
                act.activation(ev[:, b, :], ev[:, b, :], ACT.Exp, scale=-1.0).then_inc(e_done, 1)
                act.wait_ge(e_done, DB * k + b + 1)
                act.activation(lg1p[:, b, :], ev[:, b, :], ACT.Ln, bias=1.0).then_inc(l_done, 1)

            order = []

            def empty(job, k):
                if job[-1] == "<" or by_dve(job, k):
                    return
                order.append((job, k))
                src = bank_of(job, k)
                wait_filled(act, job, k)
                if job == "tn":
                    ins = act.activation(xnT[:, k % 2], src[:, :], ACT.Copy)
                elif job == "tr":
                    if k > 0:
                        act.wait_ge(filled, max(JOBS.index((other, k - 1)) for other in ("xc0", "xc1", "z0", "z1")) + 1)
                    ins = act.activation(xrT[:, :, PAD:PAD + SEQ], src[:, :].rearrange("p (b t) -> p b t", b=BPC),
                                         ACT.Copy, scale=cols[:, V_NW:V_NW + 1])
                elif job in ("z0", "z1"):
                    b = int(job[1])
                    if k == 0:
                        ins = act.activation(sz[:, k, b], src[:, :], ACT.Copy)
                    else:
                        act.wait_ge(dt_done, DB * (k - 1) + b + 1)
                        ins = act.activation(zr[:, b, :], src[:, :], ACT.Copy)
                elif job in ("xc0", "xc1"):
                    b = int(job[2])
                    if k == 0:
                        ins = act.activation(xc[:, k, b], src[:, :], ACT.Silu, bias=cols[:, V_CB + b:V_CB + b + 1])
                    else:
                        act.wait_ge(lsum_done, DB * (k - 1) + b + 1)
                        ins = act.activation(xv[:, b, :], src[:, :], ACT.Identity, bias=cols[:, V_CB + b:V_CB + b + 1])
                elif job == "dt":
                    if k > 1:
                        act.wait_ge(BC_there, 16 * NBC * (k - 1))
                    ins = act.activation(dtp[0:RANK + 2 * STATES, :], src[0:RANK + 2 * STATES, :], ACT.Copy)
                elif job == "B":
                    ins = act.activation(Bt[:, k % 2, :], src[:, :], ACT.Copy)
                elif job == "C":
                    ins = act.activation(Ct[:, k % 2, :], src[:, :], ACT.Copy)
                elif job in ("v0", "v1"):
                    b = int(job[1])
                    if k > 0:
                        act.wait_ge(corr_done, DB * (k - 1) + b + 1)
                        act.wait_ge(dt_done, DB * (k - 1) + b + 1)
                    act.activation(ev[:, b, :], src[:, :], ACT.Abs, bias=cols[:, V_BDT + b:V_BDT + b + 1])\
                        .then_inc(abs_done, 1)
                    if k == 0:
                        log1p_exp(k, b)
                    ins = act.activation(rl[:, b, :], src[:, :], ACT.Relu, bias=cols[:, V_BDT + b:V_BDT + b + 1])
                elif job == "gs":
                    ins = act.activation(sT[:, :], src[0:TPC * EXPERTS, 0:P], ACT.Copy)
                elif job[0] == "y":
                    e = int(job[1])
                    act.wait_ge(gate_step, GATE_STEPS * (k + 1))
                    if pool_experts.index((k, e)) > 0:
                        act.wait_ge(acc_added, pool_experts.index((k, e)))
                    for i in range(TPC):
                        t = slice(i * D, (i + 1) * D)
                        ins = act.activation(ysc[:, t], src[:, t], ACT.Copy, scale=score[:, k % 2, i, e:e + 1])
                elif job == "gb":
                    if k >= 3:
                        act.wait_ge(sg_done, k - 2)
                    ins = act.activation(acc[:, k % 3, :], src[:, :], ACT.Copy)
                else:
                    e, b = int(job[1]), "ab".index(job[2])
                    if e >= 2:
                        wait_filled(act, f"y{e - 2}", k)
                    elif k > 0:
                        wait_filled(act, f"y{e + EXPERTS - 2}", k - 1)
                    ins = act.activation(hT[:, e % 2, b, :], src[:, :], ACT.Relu,
                                         bias=cols[:, V_B1 + HB * e + b:V_B1 + HB * e + b + 1])
                ins.then_inc(act_emptied, 1)

            def gate_e(k):
                wait_emptied(act, "gl", k)
                act.activation(gex[:, :, :], glc[:, :, :], ACT.Exp).then_inc(gate_exp, 1)

            for job in PRE_JOBS:
                empty(job, 0)
                if job == "xc0":
                    wait_emptied(act, "xc0", 0)
                    act.activation(xc[:, 0, 0], xv[:, 0], ACT.Silu).then_inc(silu_first, 1)
                if job == "xc1":
                    act.preload_act_table_set("natural_log_exp_and_others")
                    act.activation(negA[:, :], cols[:, V_A:V_A + 32], ACT.Exp).then_inc(expA, 1)
            act.wait_ge(negated, 1)
            for n in range(LEAD):
                decay(n)
            for n in range(END_SLOT + 1):
                if n + LEAD < CHUNKS * UNITS:
                    decay(n + LEAD)
                elif n + LEAD == CHUNKS * UNITS:
                    act.preload_act_table_set("silu_and_others")
                    silu_of_experts(CHUNKS - 2)
                for k, _ in steps_at(n, "gate_e"):
                    gate_e(k)
                for k, _ in steps_at(n, "silu"):
                    silu(k)
                for job, k in SLOTS.get(n, []):
                    empty(job, k)
                for k, b in steps_at(n, "log1p"):
                    log1p_exp(k, b)
            silu_of_experts(CHUNKS - 1)
            assert order == order_a

        @block.vector
        def _(dve):
            dve.memset(xrT[:, :, 0:PAD], 0.0).then_inc(setup, 1)
            dve.memset(dtp[RANK + 2 * STATES:P, :], 0.0).then_inc(setup, 1)
            dve.memset(wdt[RANK:P, :], 0.0).then_inc(setup, 1)
            dve.memset(rsel[:, :, :], 0.0).then_inc(setup, 1)

            def stats(g):
                dve.wait_ge((x_first, x_rest)[g], 16)
                for i in NORM[g]:
                    last = dve.bn_stats(st[:, i, :], x_sb[:, i // TPC, i % TPC, :])
                last.then_inc(ln_st, 1)
                dve.wait_ge(ln_st, g + 1)
                for i in NORM[g]:
                    last = dve.bn_aggr(mv[:, i, :], st[:, i, :])
                last.then_inc(ln_mv, 1)

            def normalise(k):
                dve.wait_ge(ln_mv, min(k, 1) + 1)
                dve.wait_ge(ln_rstd, min(k, 1) + 1)
                for i in range(TPC):
                    t = TPC * k + i
                    last = dve.tensor_scalar(xn[:, k, i, :], x_sb[:, k, i, :], mv[:, t, 0:1], rstd[:, t:t + 1],
                                             ALU.subtract, ALU.mult)
                last.then_inc(ln_xn, 1)

            def scale_rows(k):
                dve.wait_ge(ln_mv, min(k, 1) + 1)
                dve.wait_ge(rms_r, min(k, 1) + 1)
                if k > 0:
                    dve.wait_ge(dt_done, DB * k)
                for i in range(TPC):
                    t = TPC * k + i
                    last = dve.tensor_scalar(xr[:, i, :], x_sb[:, k, i, :], mv[:, t, 0:1], rr[:, t:t + 1],
                                             ALU.subtract, ALU.mult)
                last.then_inc(rms_xr, 1)

            stats(0)
            scale_rows(0)
            dve.wait_ge(w_tap, 16 * N_TAP)
            for t in range(TAPS):
                dve.tensor_tensor(wtap[:, t, :], win[:, 0:DIN], cwb[:, :, t], ALU.mult).then_inc(setup, 1)
            src = bank_of("xc0", 0)[:, :].rearrange("p (b t) -> p b t", b=BPC)
            x0 = xv[:, 0].rearrange("p (b t) -> p b t", b=BPC)
            order = [("xc0", 0)]
            wait_filled(dve, "xc0", 0)
            dve.wait_ge(vec_c, 1)
            dve.tensor_scalar(x0, src, cw[:, TAPS - 1:TAPS], cols[:, V_CB:V_CB + 1], ALU.mult, ALU.add)\
                .then_inc(conv_step, 1)
            for t in range(1, TAPS):
                dve.wait_ge(conv_step, t)
                ins = dve.scalar_tensor_tensor(x0[:, :, t:], src[:, :, 0:SEQ - t], cw[:, TAPS - 1 - t:TAPS - t],
                                               x0[:, :, t:], ALU.mult, ALU.add)
                ins.then_inc(*((conv_step, 1) if t < TAPS - 1 else (dve_emptied, 1)))
            normalise(0)
            dve.wait_ge(w_proj, 16 * N_PROJ)
            for b in range(DB):
                for w, o in ((wB, RANK), (wC, RANK + STATES)):
                    dve.tensor_copy(w[:, b], wx[:, b, None, o:o + STATES].to_broadcast([P, GD, STATES]))\
                        .then_inc(setup, 1)
            dve.wait_ge(consts, 7)
            for q in range(NQ):
                dve.tensor_copy(sel_first[:, q], ident[:, 32 * q:32 * q + GD, None].to_broadcast([P, GD, STATES]))\
                    .then_inc(setup, 1)
            for p in range(3):
                s = slice(32 * p, 32 * p + 32)
                dve.tensor_copy(sel[s, :, :, :].rearrange("p g d s -> p (g d) s"),
                                ident[s, s, None].to_broadcast([32, 32, STATES])).then_inc(setup, 1)
            for g in range(GL):
                dve.tensor_copy(rsel[:, g, g * GD:(g + 1) * GD], own[:, :]).then_inc(setup, 1)

            def gate(k):
                n = [GATE_STEPS * k]

                def link(ins):
                    n[0] += 1
                    ins.then_inc(gate_step, 1)
                    dve.wait_ge(gate_step, n[0])

                src = bank_of("gl", k)[:, 0:TPC * EXPERTS].rearrange("p (t e) -> p t e", e=EXPERTS)
                wide = [P, TPC, EXPERTS]
                order.append(("gl", k))
                wait_filled(dve, "gl", k)
                link(dve.tensor_reduce(gmx[:, :], src, AX.X, ALU.max))
                dve.tensor_tensor(glc[:, :, :], src, gmx[:, :, None].to_broadcast(wide), ALU.subtract)\
                    .then_inc(dve_emptied, 1)
                yield
                dve.wait_ge(gate_exp, k + 1)
                link(dve.tensor_reduce(gsm[:, :], gex[:, :, :], AX.X, ALU.add))
                link(dve.reciprocal(gri[:, :], gsm[:, :]))
                link(dve.tensor_tensor(gp[:, :, :], gex[:, :, :], gri[:, :, None].to_broadcast(wide), ALU.mult))
                yield
                for i in range(TPC):
                    last = dve.max(gv8[:, i, :], gp[:, i, :])
                link(last)
                yield
                for i in range(TPC):
                    last = dve.max_index(gi8[:, i, :], gv8[:, i, :], gp[:, i, :])
                link(last)
                yield
                link(dve.tensor_copy(gif[:, :, :], gi8[:, :, 0:2]))
                link(dve.tensor_tensor(gs2[:, :], gv8[:, :, 0], gv8[:, :, 1], ALU.add))
                link(dve.reciprocal(grs[:, :], gs2[:, :]))
                link(dve.tensor_tensor(gvn[:, :, :], gv8[:, :, 0:2], grs[:, :, None].to_broadcast([P, TPC, 2]), ALU.mult))
                yield
                for j in range(2):
                    last = dve.tensor_tensor(goh[:, j], iota8[:, :, :], gif[:, :, j:j + 1].to_broadcast(wide), ALU.is_equal)
                link(last)
                for j in range(2):
                    last = dve.tensor_tensor(gw[:, j], goh[:, j], gvn[:, :, j:j + 1].to_broadcast(wide), ALU.mult)
                link(last)
                link(dve.tensor_tensor(score[:, k % 2], gw[:, 0], gw[:, 1], ALU.add))
                assert n[0] == GATE_STEPS * (k + 1), n[0]
                yield

            def correction(k, b, i):
                if i == 0:
                    dve.wait_ge(e_done, DB * k + b + 1)
                    dve.tensor_scalar(corr[:, b, :], ev[:, b, :], 1.0, -1.0, ALU.add, ALU.add).then_inc(round_done, 1)
                    return
                dve.wait_ge(round_done, DB * k + b + 1)
                dve.tensor_tensor(corr[:, b, :], corr[:, b, :], ev[:, b, :], ALU.subtract).then_inc(corr_done, 1)

            def times_dt(k, b):
                dve.wait_ge(dt_done, DB * k + b + 1)
                wait_silu(dve, "xc", k, b)
                dve.tensor_tensor(parts[:, b, 1, 0, :], parts[:, b, 0, 0, :], xc[:, k % 2, b], ALU.mult).then_inc(u_done, 1)
                dve.wait_ge(u_done, DB * k + b + 1)
                dve.memset(parts[:, b, 0, 0, SEQ:CH:SEQ], FAR).then_inc(far_done, 1)
                dve.wait_ge(far_done, DB * k + b + 1)

            def split(k, b, kind, p):
                if p == 0:
                    dve.wait_ge(far_done, DB * k + b + 1)
                else:
                    dve.wait_ge(r1_done, 2 * (DB * k + b) + kind + 1)
                src = parts[:, b, kind, p, :]
                up = src.bitcast(BF16).rearrange("p (t two) -> p t two", two=2)[:, :, 1]
                dve.tensor_tensor(parts[:, b, kind, p + 1, :], src, up, ALU.subtract).then_inc((r1_done, r2_done)[p], 1)

            def times_B(u):
                c = u // UNITS
                dve.wait_ge(u_spread, u + 1)
                if u >= 2:
                    dve.wait_ge(scan_done, u - 1)
                if u % UNITS == 0:
                    wait_emptied(dve, "B", 0) if c == 0 else dve.wait_ge(BC_there, 16 * NBC * c)
                dve.tensor_tensor(dbu[:, u % 2, :], pu[u % 2][:, :], Bt[:, c % 2, :], ALU.mult).then_inc(dbu_done, 1)

            def scan(u):
                dve.wait_ge(decay_done, u + 1)
                dve.wait_ge(dbu_done, u + 1)
                if u >= 3:
                    dve.wait_ge(hc_done, u - 2)
                dve.tensor_tensor_scan(hs[:, u % 3, :], dec[:, u % 3, :], dbu[:, u % 2, :], 0.0, ALU.mult, ALU.add)\
                    .then_inc(scan_done, 1)

            def sum_y(c, b):
                dve.wait_ge(reduced, UNITS // PACK * c + (b + 1) * UNITS // PACK // DB)
                if c > 0:
                    wait_filled(dve, "o", c - 1)
                dve.scalar_tensor_tensor(yg[:, b, :], xc[:, c % 2, b, :], cols[:, V_DS + b:V_DS + b + 1], py[:, :],
                                         ALU.mult, ALU.add).then_inc(y_taken, 1)

            def gate_z(c, b):
                dve.wait_ge(y_taken, DB * c + b + 1)
                wait_silu(dve, "z", c, b)
                dve.tensor_tensor(yg[:, b, :], yg[:, b, :], sz[:, c % 2, b, :], ALU.mult).then_inc(yg_done, 1)

            def empty(job, k):
                src = bank_of(job, k)
                if not by_dve(job, k) or job == "gl":
                    return
                order.append((job, k))
                wait_filled(dve, job, k)
                if job == "o":
                    dve.tensor_tensor(s_sb[:, k, :], src[:, :], xn[:, k].rearrange("p t d -> p (t d)"),
                                      ALU.add).then_inc(dve_emptied, 1)
                    return
                e = int(job[1])
                wait_added(dve, k, e - 1)
                for i in range(TPC):
                    t = slice(i * D, (i + 1) * D)
                    last = dve.scalar_tensor_tensor(acc[:, k % 3, t], src[:, t], score[:, k % 2, i, e:e + 1],
                                                    acc[:, k % 3, t], ALU.mult, ALU.add)
                last.then_inc(dve_emptied, 1)

            stats(1)
            dve.wait_ge(expA, 1)
            dve.tensor_scalar(negA[:, :], negA[:, :], -1.0, None, ALU.mult).then_inc(negated, 1)
            correction(0, 0, 0)
            correction(0, 0, 1)
            softplus_sum(dve, 0, 0)
            times_dt(0, 0)
            for kind in range(2):
                split(0, 0, kind, 0)
                split(0, 0, kind, 1)
            times_B(0)
            gates = [gate(k) for k in range(CHUNKS)]
            for n in range(END_SLOT + 2):
                if n + 1 < CHUNKS * UNITS:
                    times_B(n + 1)
                if n < CHUNKS * UNITS:
                    scan(n)
                if n == CHUNKS * UNITS - 1:
                    times_C(dve, n)
                for k, b in steps_at(n, "sum_y"):
                    sum_y(k - 1, b)
                for k, b in steps_at(n, "gate_z"):
                    gate_z(k - 1, b)
                for k, _ in steps_at(n, "scale_rows"):
                    scale_rows(k)
                for k, _ in steps_at(n, "normalise"):
                    normalise(k)
                for k, _ in steps_at(n, "gate"):
                    next(gates[k])
                for k, i in steps_at(n, "correct"):
                    correction(k, i // 2 + (k == 0), i % 2)
                for k, b in steps_at(n, "times_dt"):
                    times_dt(k, b + (k == 0))
                for p, name in enumerate(("split_1", "split_2")):
                    for k, i in steps_at(n, name):
                        split(k, i // 2 + (k == 0), i % 2, p)
                for job, k in SLOTS.get(n - 1, []):
                    empty(job, k) if job[-1] != "<" else None
            assert order == order_v
            k = CHUNKS - 1
            wait_emptied(dve, "o", k)
            dve.wait_ge(g_done, k + 1)
            dve.tensor_tensor(s_sb[:, k, :], s_sb[:, k, :], acc[:, k % 3, :], ALU.mult).then_inc(last_sg_done, 1)
            dve.wait_ge(last_sg_done, 1)
            dve.tensor_tensor(s_sb[:, k, :], s_sb[:, k, :], x_sb[:, k].rearrange("p t d -> p (t d)"),
                              ALU.add).then_inc(last_done, 1)

        @block.tensor
        def _(pe):
            pe.wait_ge(w_rows, 16 * N_ROWS)
            pe.wait_ge(consts, 7)
            pe.transpose(pd[0][:, 0:V_END], rows[:, :], ident[0:V_END, 0:V_END]).then_inc(vec_t, 1)

            def spread(u, kind):
                b, gl, q = place(u)
                if u == PACK or u % (GL * NQ) == 0 and u > 0:
                    pe.wait_ge(stacked[b], 16 * 3 * NQ * (u // UNITS + 1))
                w = sel[:, gl].rearrange("p d s -> p (d s)")
                dst, used, done = ((pd, decay_done, dt_spread), (pu, dbu_done, u_spread))[kind]
                if u >= 2:
                    pe.wait_ge(used, u - 1)
                if u < PACK:
                    pe.wait_ge(r2_done, kind + 1)
                    for part in range(3):
                        up = parts[:, b, kind, part, :].bitcast(BF16).rearrange("p (t two) -> p t two", two=2)[:, :, 1]
                        last = pe.matmul(dst[u % 2][:, :], sel_first[:, q].rearrange("p d s -> p (d s)"), up,
                                         start=part == 0, stop=part == 2)
                    last.then_inc(done, 1)
                    return
                up = stack[0:96, b, q, kind, :].bitcast(BF16).rearrange("p (t two) -> p t two", two=2)[:, :, 1]
                pe.matmul(dst[u % 2][:, :], w, up, start=True, stop=True).then_inc(done, 1)

            def reduce_pack(m):
                block_, gl = m // GL, m % GL
                pe.wait_ge(hc_done, PACK * (m + 1))
                if gl == 0 and block_ > 0:
                    pe.wait_ge(y_taken, block_)
                for q in range(NQ):
                    last = pe.matmul(py[32 * q:32 * q + 32, :], rsel[:, gl, :], hc[:, (PACK * m + q) % (2 * PACK), :],
                                     start=gl == 0, stop=gl == GL - 1)
                last.then_inc(reduced, 1)

            def fill(job, k):
                started, job = job[-1] == "<", job.rstrip("<")
                second = not started and (job, k) in STARTED
                j = JOBS.index((job, k))
                dst = px[j % AUX]
                if j >= AUX:
                    wait_emptied(pe, *JOBS[j - AUX])
                if job == "tn":
                    pe.wait_ge(ln_xn, k + 1)
                    for i in range(TPC):
                        last = pe.transpose(dst[:, i * P:(i + 1) * P], xn[:, k, i, :], ident[:, :])
                elif job == "tr":
                    pe.wait_ge(rms_xr, k + 1)
                    for i in range(TPC):
                        last = pe.transpose(dst[:, i * P:(i + 1) * P], xr[:, i, :], ident[:, :])
                elif job in ("z0", "z1"):
                    wait_emptied(pe, "tr", k)
                    if k == 0:
                        pe.wait_ge(w_tap, 16 * N_TAP)
                    o = DIN + int(job[1]) * P
                    last = pe.matmul(dst[:, :], win[:, o:o + P], xrT[:, :, PAD:PAD + SEQ], start=True, stop=True)
                elif (job, k) == ("xc0", 0):
                    wait_emptied(pe, "tr", k)
                    pe.wait_ge(w_tap, 16 * N_TAP)
                    last = pe.matmul(dst[:, :], win[:, 0:P], xrT[:, :, PAD:PAD + SEQ], start=True, stop=True)
                elif job in ("xc0", "xc1"):
                    wait_emptied(pe, "tr", k)
                    if k == 0:
                        pe.wait_ge(setup, 4 + TAPS)
                    b = int(job[2])
                    for t in (range(2) if started else range(2, TAPS) if second else range(TAPS)):
                        last = pe.matmul(dst[:, :], wtap[:, t, b * P:(b + 1) * P], xrT[:, :, t:t + SEQ],
                                         start=t == 0, stop=t == TAPS - 1)
                elif job in ("dt", "B", "C"):
                    if k == 0:
                        pe.wait_ge(setup, 4 + TAPS + 2 * DB)
                    for b in range(DB):
                        w = {"dt": wx[:, b, :], "B": wB[:, b].rearrange("p d s -> p (d s)"),
                             "C": wC[:, b].rearrange("p d s -> p (d s)")}[job]
                        wait_silu(pe, "xc", k, b)
                        last = pe.matmul(dst[0:RANK + 2 * STATES if job == "dt" else P, :], w, xc[:, k % 2, b, :],
                                         start=b == 0, stop=b == DB - 1)
                elif job in ("v0", "v1"):
                    wait_emptied(pe, "dt", k)
                    b = int(job[1])
                    pe.wait_ge(setup, 4)
                    last = pe.matmul(dst[:, :], wdt[:, b * P:(b + 1) * P], dtp[:, :], start=True, stop=True)
                elif job == "gl":
                    wait_emptied(pe, "tn", k)
                    if k == 0:
                        pe.wait_ge(w_proj, 16 * N_PROJ)
                    for i in range(TPC):
                        last = pe.matmul(dst[:, i * EXPERTS:(i + 1) * EXPERTS], xnT[:, k % 2, i * P:(i + 1) * P], wg[:, :],
                                         start=True, stop=True)
                elif job == "gs":
                    pe.wait_ge(gate_step, GATE_STEPS * (k + 1))
                    last = pe.transpose(dst[0:TPC * EXPERTS, 0:P], score[:, k % 2].rearrange("p t e -> p (t e)"),
                                        ident[:, :])
                elif job == "gb":
                    wait_emptied(pe, "gs", k)
                    if k == 0:
                        pe.wait_ge(w_moe, 16 * N_MOE)
                    last = pe.matmul(dst[:, :], sT[:, :], b2d[:, :, :].rearrange("e t d -> e (t d)"), start=True, stop=True)
                elif job[0] == "m":
                    e, b = int(job[1]), "ab".index(job[2])
                    wait_emptied(pe, "tn", k)
                    if k == 0:
                        pe.wait_ge(w_moe, 16 * N_MOE)
                    last = pe.matmul(dst[:, :], w1[:, e, b * P:(b + 1) * P], xnT[:, k % 2, :], start=True, stop=True)
                elif job[0] == "y":
                    e = int(job[1])
                    wait_all_emptied(pe, (f"m{e}a", f"m{e}b"), k)
                    for i in range(TPC // 2) if started else range(TPC // 2, TPC) if second else range(TPC):
                        for b in range(HB):
                            last = pe.matmul(dst[:, i * D:(i + 1) * D], hT[:, e % 2, b, i * P:(i + 1) * P], w2[:, e, b, :],
                                             start=b == 0, stop=b == HB - 1)
                else:
                    for b in range(DB):
                        pe.wait_ge(yg_done, DB * k + b + 1)
                        for i in range(TPC):
                            last = pe.matmul(dst[:, i * D:(i + 1) * D], yg[:, b, i * P:(i + 1) * P], wout[:, b, :],
                                             start=b + i == 0, stop=(b, i) == (DB - 1, TPC - 1))
                if not started:
                    last.then_inc(filled, 1)

            for job in PRE_JOBS:
                fill(job, 0)
            pe.wait_ge(setup, N_SETUP)
            pe.wait_ge(vec_c, 1)
            for n in range(LEAD):
                spread(n, 0)
                spread(n, 1)
            for n in range(END_SLOT + 1):
                if n + LEAD < CHUNKS * UNITS:
                    spread(n + LEAD, 0)
                    spread(n + LEAD, 1)
                if n >= LAG and (n - LAG) % PACK == PACK - 1 and n - LAG < CHUNKS * UNITS:
                    reduce_pack((n - LAG) // PACK)
                for job, k in SLOTS.get(n, []):
                    fill(job, k)


_INS = ["L0_attn_x", "L0_attn_norm_w", "L0_attn_W_in", "L0_attn_conv_w", "L0_attn_conv_b", "L0_attn_W_x",
        "L0_attn_W_dt", "L0_attn_b_dt", "L0_attn_A_log", "L0_attn_D_skip", "L0_attn_W_out",
        "L0_ffn_Wg", "L0_ffn_W1", "L0_ffn_b1", "L0_ffn_W2", "L0_ffn_b2"]


def kernel(**inputs):
    import numpy as np
    import concourse.bacc as bacc
    from concourse.bass_utils import run_bass_kernel_spmd

    nc = bacc.Bacc("TRN2", target_bir_lowering=False, num_devices=1)
    arrays, args = {}, []
    for name in _INS:
        a = np.ascontiguousarray(inputs[name])
        arrays[f"in_{name}"] = a
        args.append(nc.dram_tensor(f"in_{name}", a.shape, mybir.dt.from_np(a.dtype), kind="ExternalInput").ap())
    args.append(nc.dram_tensor("out_0", (BATCH, SEQ, D), F32, kind="ExternalOutput").ap())
    mamba_moe(nc, *args)
    r = run_bass_kernel_spmd(nc, [arrays], core_ids=[0])
    return r.results[0]["out_0"]
```
